# Optimizing a Trainium2 kernel written in Bass

```python
import numpy as np
import jax
import jax.numpy as jnp

def _softmax(x, axis=-1):
    return jax.nn.softmax(x, axis=axis)

def _gelu(x):
    return jax.nn.gelu(x, approximate=True)

def _silu(x):
    return jax.nn.silu(x)

def _sigmoid(x):
    return jax.nn.sigmoid(x)

def _layernorm(x, axis=-1, eps=1e-05):
    m = jnp.mean(x, axis=axis, keepdims=True)
    v = jnp.var(x, axis=axis, keepdims=True)
    return (x - m) / jnp.sqrt(v + eps)

def _scatter_add(tgt, idx, src, axis=0):
    return tgt.at[idx].add(src)

def _segment_sum(src, seg, n):
    return jax.ops.segment_sum(src, seg, n)
kernel_name = 'mk_xattn_seq_d4_seqx_r4_b81df8'

def setup_inputs(seed: int=0):
    np.random.seed(seed)
    _w = jnp.asarray

    def _rec_inputs():
        import jax
        import jax.numpy as jnp
        _rk = jax.random.key(seed)
        x = -0.0002928 + 1 * jax.random.normal(jax.random.fold_in(_rk, 1), (32, 256, 256), jnp.float32)
        _lenS = 256 - jax.random.randint(jax.random.fold_in(_rk, 7), (32,), 0, max(1, 256 // 4) + 1, jnp.int32)
        _lenS2 = 256 - jax.random.randint(jax.random.fold_in(_rk, 8), (32,), 0, max(1, 256 // 4) + 1, jnp.int32)
        _ctx_1024P = jax.random.normal(jax.random.fold_in(_rk, 11), (32, 16, 256), jnp.float32)
        _ctx_1024c = jax.random.dirichlet(jax.random.fold_in(_rk, 511), 0.3 * jnp.ones((16,), jnp.float32), (32, 256))
        _ctx_1024t = jnp.einsum('bsk,bkd->bsd', _ctx_1024c, _ctx_1024P)
        _ctx_1024t = _ctx_1024t * jax.lax.rsqrt(jnp.mean(jnp.square(_ctx_1024t)) + 1e-12) * 0.953939
        ctx_1024 = -1.39393e-06 + 0.999914 * (_ctx_1024t + 0.3 * jax.random.normal(jax.random.fold_in(_rk, 611), (32, 256, 256), jnp.float32))
        _validS = jnp.arange(256)[None, :] < _lenS[:, None]
        _validS2 = jnp.arange(256)[None, :] < _lenS2[:, None]
        _causal = jnp.tril(jnp.ones((256, 256), dtype=bool))
        mask_BxSxS2_bf0 = jnp.logical_not(jnp.ones((32, 256, 256), dtype=bool))
        mask_Bx1x1xS2_if1 = jnp.where(jnp.ones((32, 1, 1, 256), dtype=bool), 1, 0).astype(jnp.int32)
        mask_1x1xSxS_bk0 = jnp.logical_not(jnp.broadcast_to(_validS[0:1, None, None, :], (1, 1, 256, 256)))
        return (x, ctx_1024, mask_BxSxS2_bf0, mask_Bx1x1xS2_if1, mask_1x1xSxS_bk0)
    x, ctx_1024, mask_BxSxS2_bf0, mask_Bx1x1xS2_if1, mask_1x1xSxS_bk0 = _rec_inputs()

    def _L0_xattn_setup():
        import jax, jax.numpy as jnp
        import numpy as np
        B, S, D_MODEL, H, DH = (2, 512, 256, 16, 64)
        LN_EPS = 1e-05
        key = jax.random.key(seed)
        ks = jax.random.split(key, 12)
        sc_in = 1.0 / np.sqrt(D_MODEL)
        sc_hd = 1.0 / np.sqrt(H * DH)
        return {'Q': jax.random.normal(ks[0], (B, S, D_MODEL), jnp.float32), 'K': jax.random.normal(ks[1], (B, S, D_MODEL), jnp.float32), 'V': jax.random.normal(ks[2], (B, S, D_MODEL), jnp.float32), 'attn_mask': jnp.zeros((B, S, S), dtype=bool), 'Wq': jax.random.normal(ks[3], (D_MODEL, H * DH), jnp.float32) * sc_in, 'bq': jax.random.normal(ks[4], (H * DH,), jnp.float32) * 0.01, 'Wk': jax.random.normal(ks[5], (D_MODEL, H * DH), jnp.float32) * sc_in, 'bk': jax.random.normal(ks[6], (H * DH,), jnp.float32) * 0.01, 'Wv': jax.random.normal(ks[7], (D_MODEL, H * DH), jnp.float32) * sc_in, 'bv': jax.random.normal(ks[8], (H * DH,), jnp.float32) * 0.01, 'Wo': jax.random.normal(ks[9], (H * DH, D_MODEL), jnp.float32) * sc_hd, 'bo': jax.random.normal(ks[10], (D_MODEL,), jnp.float32) * 0.01, 'gamma': jnp.ones((D_MODEL,), jnp.float32), 'beta': jnp.zeros((D_MODEL,), jnp.float32)}
    _L0_xattn_all = _L0_xattn_setup()
    _L0_xattn_in = {k: v for k, v in _L0_xattn_all.items() if k in ('Wq', 'bq', 'Wk', 'bk', 'Wv', 'bv', 'Wo', 'bo', 'gamma', 'beta')}
    del _L0_xattn_all

    def _L1_xattn_setup():
        import jax, jax.numpy as jnp
        import numpy as np
        EMBED = 256
        HEADS = 16
        HEAD_DIM = EMBED // HEADS
        FF = 4 * EMBED
        EPS = 1e-05

        def layernorm(x, g, b):
            mu = jnp.mean(x, axis=-1, keepdims=True)
            var = jnp.mean((x - mu) ** 2, axis=-1, keepdims=True)
            return (x - mu) * jax.lax.rsqrt(var + EPS) * g + b
        key = jax.random.key(seed)
        ks = jax.random.split(key, 16)
        B, S = (2, 512)
        f32 = jnp.float32
        inp = {'value': jax.random.normal(ks[0], (B, S, EMBED), f32), 'key': jax.random.normal(ks[1], (B, S, EMBED), f32), 'query': jax.random.normal(ks[2], (B, S, EMBED), f32), 'mask': jnp.ones((B, 1, 1, S), jnp.int32), 'wv': jax.random.normal(ks[3], (HEAD_DIM, HEAD_DIM), f32) * 0.02, 'wk': jax.random.normal(ks[4], (HEAD_DIM, HEAD_DIM), f32) * 0.02, 'wq': jax.random.normal(ks[5], (HEAD_DIM, HEAD_DIM), f32) * 0.02, 'w_out': jax.random.normal(ks[6], (EMBED, EMBED), f32) * 0.02, 'b_out': jnp.zeros((EMBED,), f32), 'g1': jnp.ones((EMBED,), f32), 'beta1': jnp.zeros((EMBED,), f32), 'w_ff1': jax.random.normal(ks[7], (EMBED, FF), f32) * 0.02, 'b_ff1': jnp.zeros((FF,), f32), 'w_ff2': jax.random.normal(ks[8], (FF, EMBED), f32) * 0.02, 'b_ff2': jnp.zeros((EMBED,), f32), 'g2': jnp.ones((EMBED,), f32), 'beta2': jnp.zeros((EMBED,), f32)}
        return inp
    _L1_xattn_all = _L1_xattn_setup()
    _L1_xattn_in = {k: v for k, v in _L1_xattn_all.items() if k in ('wv', 'wk', 'wq', 'w_out', 'b_out', 'g1', 'beta1', 'w_ff1', 'b_ff1', 'w_ff2', 'b_ff2', 'g2', 'beta2')}
    del _L1_xattn_all

    def _L2_xattn_setup():
        import jax, jax.numpy as jnp
        import numpy as np
        D_MODEL = 256
        N_HEADS = 16
        D_K = D_MODEL // N_HEADS
        LN_EPS = 1e-05

        def _attention(query, key_value, W_qkv, b_qkv, W_o, b_o, ln_gamma, ln_beta):
            B, Sq, _ = query.shape
            Skv = key_value.shape[1]
            Wq, Wk, Wv = (W_qkv[:D_MODEL], W_qkv[D_MODEL:2 * D_MODEL], W_qkv[2 * D_MODEL:])
            bq, bk, bv = (b_qkv[:D_MODEL], b_qkv[D_MODEL:2 * D_MODEL], b_qkv[2 * D_MODEL:])
            Q = (query @ Wq.T + bq).reshape(B, Sq, N_HEADS, D_K).transpose(0, 2, 1, 3)
            K = (key_value @ Wk.T + bk).reshape(B, Skv, N_HEADS, D_K).transpose(0, 2, 1, 3)
            V = (key_value @ Wv.T + bv).reshape(B, Skv, N_HEADS, D_K).transpose(0, 2, 1, 3)
            scores = jnp.einsum('bhqd,bhkd->bhqk', Q.astype(jnp.float32), K.astype(jnp.float32))
            scores = scores / np.sqrt(D_K)
            attn = jax.nn.softmax(scores, axis=-1)
            context = jnp.einsum('bhqk,bhkd->bhqd', attn, V.astype(jnp.float32)).astype(query.dtype)
            context = context.transpose(0, 2, 1, 3).reshape(B, Sq, D_MODEL)
            output = context @ W_o.T + b_o
            x = output + query
            mu = jnp.mean(x, axis=-1, keepdims=True)
            var = jnp.mean(jnp.square(x - mu), axis=-1, keepdims=True)
            return (x - mu) / jnp.sqrt(var + LN_EPS) * ln_gamma + ln_beta
        key = jax.random.key(seed)
        ks = jax.random.split(key, 8)
        B, Sq, Skv = (2, 512, 512)
        scale = 1.0 / np.sqrt(D_MODEL)
        return {'query': jax.random.normal(ks[0], (B, Sq, D_MODEL), dtype=jnp.float32), 'key_value': jax.random.normal(ks[1], (B, Skv, D_MODEL), dtype=jnp.float32), 'W_qkv': jax.random.normal(ks[2], (3 * D_MODEL, D_MODEL), dtype=jnp.float32) * scale, 'b_qkv': jax.random.normal(ks[3], (3 * D_MODEL,), dtype=jnp.float32) * 0.01, 'W_o': jax.random.normal(ks[4], (D_MODEL, D_MODEL), dtype=jnp.float32) * scale, 'b_o': jax.random.normal(ks[5], (D_MODEL,), dtype=jnp.float32) * 0.01, 'ln_gamma': jnp.ones((D_MODEL,), dtype=jnp.float32), 'ln_beta': jnp.zeros((D_MODEL,), dtype=jnp.float32)}
    _L2_xattn_all = _L2_xattn_setup()
    _L2_xattn_in = {k: v for k, v in _L2_xattn_all.items() if k in ('W_qkv', 'b_qkv', 'W_o', 'b_o', 'ln_gamma', 'ln_beta')}
    del _L2_xattn_all

    def _L3_xattn_setup():
        import jax, jax.numpy as jnp
        import numpy as np
        EMBED_DIM = 256
        NUM_HEADS = 16
        HEAD_DIM = EMBED_DIM // NUM_HEADS
        FF_DIM = 1024
        B, T, S = (2, 512, 512)
        LN_EPS = 1e-05

        def _layernorm(x, g, b):
            mu = jnp.mean(x, -1, keepdims=True)
            var = jnp.mean(jnp.square(x - mu), -1, keepdims=True)
            return (x - mu) * jax.lax.rsqrt(var + LN_EPS) * g + b

        def _mha(q_in, k_in, v_in, wq, bq, wk, bk, wv, bv, wo, bo, mask=None):
            Bq, Tq, C = q_in.shape
            Tk = k_in.shape[1]
            Q = (q_in @ wq + bq).reshape(Bq, Tq, NUM_HEADS, HEAD_DIM)
            K = (k_in @ wk + bk).reshape(Bq, Tk, NUM_HEADS, HEAD_DIM)
            V = (v_in @ wv + bv).reshape(Bq, Tk, NUM_HEADS, HEAD_DIM)
            scores = jnp.einsum('bqhd,bkhd->bhqk', Q, K) / np.sqrt(HEAD_DIM)
            if mask is not None:
                scores = jnp.where(mask, scores, -jnp.inf)
            attn = jax.nn.softmax(scores, axis=-1)
            out = jnp.einsum('bhqk,bkhd->bqhd', attn, V).reshape(Bq, Tq, C)
            return out @ wo + bo
        key = jax.random.key(seed)
        ks = jax.random.split(key, 20)
        sd = 1.0 / np.sqrt(EMBED_DIM)
        d = {'x': jax.random.normal(ks[0], (B, T, EMBED_DIM), jnp.float32), 'encoder_outputs': jax.random.normal(ks[1], (B, S, EMBED_DIM), jnp.float32), 'tgt_mask': jnp.tril(jnp.ones((T, T), bool))[None, None]}
        names = ['sa_wq', 'sa_wk', 'sa_wv', 'sa_wo', 'ca_wq', 'ca_wk', 'ca_wv', 'ca_wo']
        for i, n in enumerate(names):
            d[n] = jax.random.normal(ks[2 + i], (EMBED_DIM, EMBED_DIM), jnp.float32) * sd
            d[n.replace('w', 'b')] = jnp.zeros((EMBED_DIM,), jnp.float32)
        d['ff_w1'] = jax.random.normal(ks[10], (EMBED_DIM, FF_DIM), jnp.float32) * sd
        d['ff_b1'] = jnp.zeros((FF_DIM,), jnp.float32)
        d['ff_w2'] = jax.random.normal(ks[11], (FF_DIM, EMBED_DIM), jnp.float32) * (1.0 / np.sqrt(FF_DIM))
        d['ff_b2'] = jnp.zeros((EMBED_DIM,), jnp.float32)
        for i in (1, 2, 3):
            d[f'ln{i}_g'] = jnp.ones((EMBED_DIM,), jnp.float32)
            d[f'ln{i}_b'] = jnp.zeros((EMBED_DIM,), jnp.float32)
        return d
    _L3_xattn_all = _L3_xattn_setup()
    _L3_xattn_in = {k: v for k, v in _L3_xattn_all.items() if k in ('sa_wq', 'sa_bq', 'sa_wk', 'sa_bk', 'sa_wv', 'sa_bv', 'sa_wo', 'sa_bo', 'ca_wq', 'ca_bq', 'ca_wk', 'ca_bk', 'ca_wv', 'ca_bv', 'ca_wo', 'ca_bo', 'ff_w1', 'ff_b1', 'ff_w2', 'ff_b2', 'ln1_g', 'ln1_b', 'ln2_g', 'ln2_b', 'ln3_g', 'ln3_b')}
    del _L3_xattn_all
    return {'x': x, 'ctx_1024': ctx_1024, 'mask_BxSxS2_bf0': mask_BxSxS2_bf0, 'mask_Bx1x1xS2_if1': mask_Bx1x1xS2_if1, 'mask_1x1xSxS_bk0': mask_1x1xSxS_bk0, 'L0_xattn_Wq': _L0_xattn_in['Wq'], 'L0_xattn_bq': _L0_xattn_in['bq'], 'L0_xattn_Wk': _L0_xattn_in['Wk'], 'L0_xattn_bk': _L0_xattn_in['bk'], 'L0_xattn_Wv': _L0_xattn_in['Wv'], 'L0_xattn_bv': _L0_xattn_in['bv'], 'L0_xattn_Wo': _L0_xattn_in['Wo'], 'L0_xattn_bo': _L0_xattn_in['bo'], 'L0_xattn_gamma': _L0_xattn_in['gamma'], 'L0_xattn_beta': _L0_xattn_in['beta'], 'L1_xattn_wv': _L1_xattn_in['wv'], 'L1_xattn_wk': _L1_xattn_in['wk'], 'L1_xattn_wq': _L1_xattn_in['wq'], 'L1_xattn_w_out': _L1_xattn_in['w_out'], 'L1_xattn_b_out': _L1_xattn_in['b_out'], 'L1_xattn_g1': _L1_xattn_in['g1'], 'L1_xattn_beta1': _L1_xattn_in['beta1'], 'L1_xattn_w_ff1': _L1_xattn_in['w_ff1'], 'L1_xattn_b_ff1': _L1_xattn_in['b_ff1'], 'L1_xattn_w_ff2': _L1_xattn_in['w_ff2'], 'L1_xattn_b_ff2': _L1_xattn_in['b_ff2'], 'L1_xattn_g2': _L1_xattn_in['g2'], 'L1_xattn_beta2': _L1_xattn_in['beta2'], 'L2_xattn_W_qkv': _L2_xattn_in['W_qkv'], 'L2_xattn_b_qkv': _L2_xattn_in['b_qkv'], 'L2_xattn_W_o': _L2_xattn_in['W_o'], 'L2_xattn_b_o': _L2_xattn_in['b_o'], 'L2_xattn_ln_gamma': _L2_xattn_in['ln_gamma'], 'L2_xattn_ln_beta': _L2_xattn_in['ln_beta'], 'L3_xattn_sa_wq': _L3_xattn_in['sa_wq'], 'L3_xattn_sa_bq': _L3_xattn_in['sa_bq'], 'L3_xattn_sa_wk': _L3_xattn_in['sa_wk'], 'L3_xattn_sa_bk': _L3_xattn_in['sa_bk'], 'L3_xattn_sa_wv': _L3_xattn_in['sa_wv'], 'L3_xattn_sa_bv': _L3_xattn_in['sa_bv'], 'L3_xattn_sa_wo': _L3_xattn_in['sa_wo'], 'L3_xattn_sa_bo': _L3_xattn_in['sa_bo'], 'L3_xattn_ca_wq': _L3_xattn_in['ca_wq'], 'L3_xattn_ca_bq': _L3_xattn_in['ca_bq'], 'L3_xattn_ca_wk': _L3_xattn_in['ca_wk'], 'L3_xattn_ca_bk': _L3_xattn_in['ca_bk'], 'L3_xattn_ca_wv': _L3_xattn_in['ca_wv'], 'L3_xattn_ca_bv': _L3_xattn_in['ca_bv'], 'L3_xattn_ca_wo': _L3_xattn_in['ca_wo'], 'L3_xattn_ca_bo': _L3_xattn_in['ca_bo'], 'L3_xattn_ff_w1': _L3_xattn_in['ff_w1'], 'L3_xattn_ff_b1': _L3_xattn_in['ff_b1'], 'L3_xattn_ff_w2': _L3_xattn_in['ff_w2'], 'L3_xattn_ff_b2': _L3_xattn_in['ff_b2'], 'L3_xattn_ln1_g': _L3_xattn_in['ln1_g'], 'L3_xattn_ln1_b': _L3_xattn_in['ln1_b'], 'L3_xattn_ln2_g': _L3_xattn_in['ln2_g'], 'L3_xattn_ln2_b': _L3_xattn_in['ln2_b'], 'L3_xattn_ln3_g': _L3_xattn_in['ln3_g'], 'L3_xattn_ln3_b': _L3_xattn_in['ln3_b']}

def reference(x, ctx_1024, mask_BxSxS2_bf0, mask_Bx1x1xS2_if1, mask_1x1xSxS_bk0, L0_xattn_Wq, L0_xattn_bq, L0_xattn_Wk, L0_xattn_bk, L0_xattn_Wv, L0_xattn_bv, L0_xattn_Wo, L0_xattn_bo, L0_xattn_gamma, L0_xattn_beta, L1_xattn_wv, L1_xattn_wk, L1_xattn_wq, L1_xattn_w_out, L1_xattn_b_out, L1_xattn_g1, L1_xattn_beta1, L1_xattn_w_ff1, L1_xattn_b_ff1, L1_xattn_w_ff2, L1_xattn_b_ff2, L1_xattn_g2, L1_xattn_beta2, L2_xattn_W_qkv, L2_xattn_b_qkv, L2_xattn_W_o, L2_xattn_b_o, L2_xattn_ln_gamma, L2_xattn_ln_beta, L3_xattn_sa_wq, L3_xattn_sa_bq, L3_xattn_sa_wk, L3_xattn_sa_bk, L3_xattn_sa_wv, L3_xattn_sa_bv, L3_xattn_sa_wo, L3_xattn_sa_bo, L3_xattn_ca_wq, L3_xattn_ca_bq, L3_xattn_ca_wk, L3_xattn_ca_bk, L3_xattn_ca_wv, L3_xattn_ca_bv, L3_xattn_ca_wo, L3_xattn_ca_bo, L3_xattn_ff_w1, L3_xattn_ff_b1, L3_xattn_ff_w2, L3_xattn_ff_b2, L3_xattn_ln1_g, L3_xattn_ln1_b, L3_xattn_ln2_g, L3_xattn_ln2_b, L3_xattn_ln3_g, L3_xattn_ln3_b):
    import jax
    import jax.numpy as jnp

    def _L0_xattn_ref(Q, K, V, attn_mask, Wq, bq, Wk, bk, Wv, bv, Wo, bo, gamma, beta):
        import jax, jax.numpy as jnp
        import numpy as np
        B, S, D_MODEL, H, DH = (2, 512, 256, 16, 64)
        LN_EPS = 1e-05
        b, s, _ = Q.shape
        q = (Q @ Wq + bq).reshape(b, s, H, DH).transpose(0, 2, 1, 3)
        k = (K @ Wk + bk).reshape(b, s, H, DH).transpose(0, 2, 1, 3)
        v = (V @ Wv + bv).reshape(b, s, H, DH).transpose(0, 2, 1, 3)
        scale = 1.0 / jnp.sqrt(jnp.asarray(DH, q.dtype))
        scores = jnp.einsum('bhqd,bhkd->bhqk', q, k) * scale
        scores = jnp.where(attn_mask[:, None, :, :], jnp.asarray(-1000000000.0, scores.dtype), scores)
        attn = jax.nn.softmax(scores, axis=-1)
        ctx = jnp.einsum('bhqk,bhkd->bhqd', attn, v)
        ctx = ctx.transpose(0, 2, 1, 3).reshape(b, s, H * DH)
        out = ctx @ Wo + bo + Q
        mu = jnp.mean(out, axis=-1, keepdims=True)
        var = jnp.var(out, axis=-1, keepdims=True)
        return (out - mu) * jax.lax.rsqrt(var + LN_EPS) * gamma + beta

    def _L1_xattn_ref(value, key, query, mask, wv, wk, wq, w_out, b_out, g1, beta1, w_ff1, b_ff1, w_ff2, b_ff2, g2, beta2):
        import jax, jax.numpy as jnp
        import numpy as np
        EMBED = 256
        HEADS = 16
        HEAD_DIM = EMBED // HEADS
        FF = 4 * EMBED
        EPS = 1e-05

        def layernorm(x, g, b):
            mu = jnp.mean(x, axis=-1, keepdims=True)
            var = jnp.mean((x - mu) ** 2, axis=-1, keepdims=True)
            return (x - mu) * jax.lax.rsqrt(var + EPS) * g + b
        B, S, E = query.shape
        v = value.reshape(B, -1, HEADS, HEAD_DIM) @ wv
        k = key.reshape(B, -1, HEADS, HEAD_DIM) @ wk
        q = query.reshape(B, -1, HEADS, HEAD_DIM) @ wq
        scores = jnp.einsum('bqhd,bkhd->bhqk', q, k)
        scores = jnp.where(mask == 0, jnp.float32(-1e+20), scores)
        attn = jax.nn.softmax(scores / jnp.sqrt(jnp.float32(EMBED)), axis=-1)
        out = jnp.einsum('bhqk,bkhd->bqhd', attn, v).reshape(B, S, E)
        attention = out @ w_out + b_out
        x = layernorm(attention + query, g1, beta1)
        ff = jax.nn.relu(x @ w_ff1 + b_ff1) @ w_ff2 + b_ff2
        return layernorm(ff + x, g2, beta2)

    def _L2_xattn_ref(query, key_value, W_qkv, b_qkv, W_o, b_o, ln_gamma, ln_beta):
        import jax, jax.numpy as jnp
        import numpy as np
        D_MODEL = 256
        N_HEADS = 16
        D_K = D_MODEL // N_HEADS
        LN_EPS = 1e-05

        def _attention(query, key_value, W_qkv, b_qkv, W_o, b_o, ln_gamma, ln_beta):
            B, Sq, _ = query.shape
            Skv = key_value.shape[1]
            Wq, Wk, Wv = (W_qkv[:D_MODEL], W_qkv[D_MODEL:2 * D_MODEL], W_qkv[2 * D_MODEL:])
            bq, bk, bv = (b_qkv[:D_MODEL], b_qkv[D_MODEL:2 * D_MODEL], b_qkv[2 * D_MODEL:])
            Q = (query @ Wq.T + bq).reshape(B, Sq, N_HEADS, D_K).transpose(0, 2, 1, 3)
            K = (key_value @ Wk.T + bk).reshape(B, Skv, N_HEADS, D_K).transpose(0, 2, 1, 3)
            V = (key_value @ Wv.T + bv).reshape(B, Skv, N_HEADS, D_K).transpose(0, 2, 1, 3)
            scores = jnp.einsum('bhqd,bhkd->bhqk', Q.astype(jnp.float32), K.astype(jnp.float32))
            scores = scores / np.sqrt(D_K)
            attn = jax.nn.softmax(scores, axis=-1)
            context = jnp.einsum('bhqk,bhkd->bhqd', attn, V.astype(jnp.float32)).astype(query.dtype)
            context = context.transpose(0, 2, 1, 3).reshape(B, Sq, D_MODEL)
            output = context @ W_o.T + b_o
            x = output + query
            mu = jnp.mean(x, axis=-1, keepdims=True)
            var = jnp.mean(jnp.square(x - mu), axis=-1, keepdims=True)
            return (x - mu) / jnp.sqrt(var + LN_EPS) * ln_gamma + ln_beta
        return _attention(query, key_value, W_qkv, b_qkv, W_o, b_o, ln_gamma, ln_beta)

    def _L3_xattn_ref(x, encoder_outputs, tgt_mask, sa_wq, sa_bq, sa_wk, sa_bk, sa_wv, sa_bv, sa_wo, sa_bo, ca_wq, ca_bq, ca_wk, ca_bk, ca_wv, ca_bv, ca_wo, ca_bo, ff_w1, ff_b1, ff_w2, ff_b2, ln1_g, ln1_b, ln2_g, ln2_b, ln3_g, ln3_b):
        import jax, jax.numpy as jnp
        import numpy as np
        EMBED_DIM = 256
        NUM_HEADS = 16
        HEAD_DIM = EMBED_DIM // NUM_HEADS
        FF_DIM = 1024
        B, T, S = (2, 512, 512)
        LN_EPS = 1e-05

        def _layernorm(x, g, b):
            mu = jnp.mean(x, -1, keepdims=True)
            var = jnp.mean(jnp.square(x - mu), -1, keepdims=True)
            return (x - mu) * jax.lax.rsqrt(var + LN_EPS) * g + b

        def _mha(q_in, k_in, v_in, wq, bq, wk, bk, wv, bv, wo, bo, mask=None):
            Bq, Tq, C = q_in.shape
            Tk = k_in.shape[1]
            Q = (q_in @ wq + bq).reshape(Bq, Tq, NUM_HEADS, HEAD_DIM)
            K = (k_in @ wk + bk).reshape(Bq, Tk, NUM_HEADS, HEAD_DIM)
            V = (v_in @ wv + bv).reshape(Bq, Tk, NUM_HEADS, HEAD_DIM)
            scores = jnp.einsum('bqhd,bkhd->bhqk', Q, K) / np.sqrt(HEAD_DIM)
            if mask is not None:
                scores = jnp.where(mask, scores, -jnp.inf)
            attn = jax.nn.softmax(scores, axis=-1)
            out = jnp.einsum('bhqk,bkhd->bqhd', attn, V).reshape(Bq, Tq, C)
            return out @ wo + bo
        h = _layernorm(x, ln1_g, ln1_b)
        x = x + _mha(h, h, h, sa_wq, sa_bq, sa_wk, sa_bk, sa_wv, sa_bv, sa_wo, sa_bo, tgt_mask)
        h = _layernorm(x, ln2_g, ln2_b)
        x = x + _mha(h, encoder_outputs, encoder_outputs, ca_wq, ca_bq, ca_wk, ca_bk, ca_wv, ca_bv, ca_wo, ca_bo, None)
        h = _layernorm(x, ln3_g, ln3_b)
        ff = jax.nn.relu(h @ ff_w1 + ff_b1) @ ff_w2 + ff_b2
        return x + ff
    x = _L0_xattn_ref(x, ctx_1024, ctx_1024, mask_BxSxS2_bf0, L0_xattn_Wq, L0_xattn_bq, L0_xattn_Wk, L0_xattn_bk, L0_xattn_Wv, L0_xattn_bv, L0_xattn_Wo, L0_xattn_bo, L0_xattn_gamma, L0_xattn_beta)
    x = _L1_xattn_ref(ctx_1024, ctx_1024, x, mask_Bx1x1xS2_if1, L1_xattn_wv, L1_xattn_wk, L1_xattn_wq, L1_xattn_w_out, L1_xattn_b_out, L1_xattn_g1, L1_xattn_beta1, L1_xattn_w_ff1, L1_xattn_b_ff1, L1_xattn_w_ff2, L1_xattn_b_ff2, L1_xattn_g2, L1_xattn_beta2)
    x = _L2_xattn_ref(x, ctx_1024, L2_xattn_W_qkv, L2_xattn_b_qkv, L2_xattn_W_o, L2_xattn_b_o, L2_xattn_ln_gamma, L2_xattn_ln_beta)
    x = _L3_xattn_ref(x, ctx_1024, mask_1x1xSxS_bk0, L3_xattn_sa_wq, L3_xattn_sa_bq, L3_xattn_sa_wk, L3_xattn_sa_bk, L3_xattn_sa_wv, L3_xattn_sa_bv, L3_xattn_sa_wo, L3_xattn_sa_bo, L3_xattn_ca_wq, L3_xattn_ca_bq, L3_xattn_ca_wk, L3_xattn_ca_bk, L3_xattn_ca_wv, L3_xattn_ca_bv, L3_xattn_ca_wo, L3_xattn_ca_bo, L3_xattn_ff_w1, L3_xattn_ff_b1, L3_xattn_ff_w2, L3_xattn_ff_b2, L3_xattn_ln1_g, L3_xattn_ln1_b, L3_xattn_ln2_g, L3_xattn_ln2_b, L3_xattn_ln3_g, L3_xattn_ln3_b)
    return x

_drawn_inputs = setup_inputs


def setup_inputs(seed=0):
    import zlib

    import numpy as np

    out = dict(_drawn_inputs(seed))
    spreads = {'L0_xattn_gamma': (1.0, 0.2),
     'L0_xattn_beta': (0.0, 0.1),
     'L1_xattn_b_out': (0.0, 0.1),
     'L1_xattn_g1': (1.0, 0.2),
     'L1_xattn_beta1': (0.0, 0.1),
     'L1_xattn_b_ff1': (0.0, 0.1),
     'L1_xattn_b_ff2': (0.0, 0.1),
     'L1_xattn_g2': (1.0, 0.2),
     'L1_xattn_beta2': (0.0, 0.1),
     'L2_xattn_ln_gamma': (1.0, 0.2),
     'L2_xattn_ln_beta': (0.0, 0.1),
     'L3_xattn_sa_bq': (0.0, 0.602),
     'L3_xattn_sa_bk': (0.0, 2.0),
     'L3_xattn_sa_bv': (0.0, 0.1),
     'L3_xattn_sa_bo': (0.0, 0.1),
     'L3_xattn_ca_bq': (0.0, 0.471),
     'L3_xattn_ca_bk': (0.0, 2.0),
     'L3_xattn_ca_bv': (0.0, 0.1),
     'L3_xattn_ca_bo': (0.0, 0.1),
     'L3_xattn_ff_b1': (0.0, 0.1),
     'L3_xattn_ff_b2': (0.0, 0.1),
     'L3_xattn_ln1_g': (1.0, 0.2),
     'L3_xattn_ln1_b': (0.0, 0.1),
     'L3_xattn_ln2_g': (1.0, 0.2),
     'L3_xattn_ln2_b': (0.0, 0.432),
     'L3_xattn_ln3_g': (1.0, 0.2),
     'L3_xattn_ln3_b': (0.0, 0.1)}
    factors = {'L0_xattn_bq': 36.645,
     'L0_xattn_bk': 64.0,
     'L0_xattn_bv': 7.701,
     'L0_xattn_bo': 7.269,
     'L1_xattn_wv': 5.142,
     'L1_xattn_wk': 37.414,
     'L1_xattn_wq': 37.983,
     'L1_xattn_w_out': 5.222,
     'L2_xattn_b_qkv': 5.244,
     'L2_xattn_b_o': 6.032}
    for name, (base, spread) in spreads.items():
        noise = np.random.default_rng([zlib.crc32(name.encode()), seed]).standard_normal(out[name].shape)
        drawn = base * np.exp(spread * noise) if base else spread * noise
        out[name] = jnp.asarray(drawn.astype(out[name].dtype))
    for name, factor in factors.items():
        out[name] = (out[name] * factor).astype(out[name].dtype)
    return out
```

```python
from contextlib import ExitStack
from collections import namedtuple

import numpy as np
import concourse.bass as bass
from concourse import mybir

F32 = mybir.dt.float32
F32R = mybir.dt.float32r
BF16 = mybir.dt.bfloat16
ALU = mybir.AluOpType
ACT = mybir.ActivationFunctionType
AX_X = mybir.AxisListType.X

P = 128
B, S, D = 32, 256, 256
KT = D // P
QT = S // P
STREAMS = 2
TURNS = B // STREAMS
H = 16
H0 = H // 2
PAIRS = H // 2
FT = 1024 // P
EPS = 1e-5
BIG = float(2 ** 100)
SLOT0 = 66
SLOT = 32

L0A, L0B, L1, L2, SA, CA = range(6)
PASSES = 6
SCALE = {L0A: 0.125, L0B: 0.125, L1: 0.0625, L2: 0.25, SA: 0.25, CA: 0.25}

Step = namedtuple("Step", "kind s a n u e g l")

USES = {"CT": 1, "XT": 1, "PEN": 1, "K0": 2, "Q0": 2, "V0": 2, "K": 1, "Q": 1, "V": 1, "X": 1, "MT": 1,
        "N": 1, "T0": 1, "T": 1, "O": 1, "LNa": 1, "LNb": 1, "F1": 1, "F2": 1, "OUT": 1}


def units(a):
    return H0 // 2 if a < L1 else PAIRS


def groups_after(a, n):
    if a < L1:
        return n
    return n // 2 if n % 2 else None


def attend(s, a):
    out = []
    last = units(a) - 1
    for n in range(last + 2):
        out.append(("E", s, a, n) if n <= last else ("EL", s, a, n))
        if n >= 1 and groups_after(a, n - 1) is not None:
            g = groups_after(a, n - 1)
            out.append(("N", s, a, g))
            if a < L1:
                out.append(("T0", s, a, g))
    return out


def norm(s, v):
    return [("LNa", s, v, 0), ("LNb", s, v, 0)]


def feed(s, v):
    return [("F1", s, v, n) for n in range(FT // 2)] + [("F2", s, v, 0)]


def prepare(s, a):
    out = []
    if a == L0A:
        out += [("CT", s, a, 0), ("XT", s, a, 0), ("PEN", s, a, 0)]
    if a in (L0A, L0B):
        out += [("K0", s, a, 0), ("Q0", s, a, 0), ("V0", s, a, 0)]
        tiles = units(a)
    else:
        if a == L1:
            out += [("O", s, a - 1, 0)] + norm(s, 0)
        elif a == L2:
            out += [("T", s, a - 1, 0), ("O", s, a - 1, 0)] + norm(s, 1) + feed(s, 1) + norm(s, 2)
        elif a == SA:
            out += [("T", s, a - 1, 0), ("O", s, a - 1, 0)] + norm(s, 3) + norm(s, 4)
        else:
            out += [("T", s, a - 1, 0), ("O", s, a - 1, 0)] + norm(s, 5)
        out += [("K", s, a, 0), ("Q", s, a, 0), ("V", s, a, 0)]
        tiles = PAIRS
    out += [("X", s, a, n) for n in range(QT * tiles)]
    out += [("MT", s, a, 0)]
    return out


def finish(s):
    return [("T", s, CA, 0), ("O", s, CA, 0)] + norm(s, 6) + feed(s, 6) + [("OUT", s, CA, 0)]


def merge(main, other):
    if not main or not other:
        return main + other
    out, m = [], 0
    for i, step in enumerate(other):
        while m < len(main) and (m + 0.5) * len(other) <= i * len(main):
            out.append(main[m])
            m += 1
        out.append(step)
    return out + main[m:]


def schedule():
    raw = prepare(0, 0)
    for a in range(PASSES):
        raw += merge(attend(0, a), prepare(1, a))
        raw += merge(attend(1, a), prepare(0, a + 1) if a + 1 < PASSES else finish(0))
    raw += finish(1)
    steps, u, e, g, l = [], 0, 0, 0, 0
    for kind, s, a, n in raw:
        steps.append(Step(kind, s, a, n, u, e, g, l))
        u += USES.get(kind, 0)
        e += kind == "E"
        g += kind == "N"
        l += kind == "LNa"
    return steps, u, e, g, l


STEPS, N_USES, N_UNITS, N_GROUPS, N_NORMS = schedule()
assert N_USES % 2 == 0 and N_UNITS % 2 == 0 and N_GROUPS % 2 == 0
UNIT_NO = {(t.s, t.a, t.n): t.e for t in STEPS if t.kind == "E"}
GROUP_NO = {(t.s, t.a, t.n): t.g for t in STEPS if t.kind == "N"}

LAST_USE = {(t.kind, t.s, t.a, t.n): t.u + USES[t.kind] - 1 for t in STEPS if t.kind in USES}

KQ_OPS = {L0A: 0, L0B: 4, L1: 8, L2: 10, SA: 12, CA: 14}
K_DMAS = {L1: 13, L2: 12, SA: 12, CA: 12}
M_DMAS = {L1: 3, L2: 2, SA: 2, CA: 2}
Q_DMAS = 13
SUMMED_BY = {0: lambda s: ("O", s, L0B), 1: lambda s: ("O", s, L1), 2: lambda s: ("F2", s, 1),
             3: lambda s: ("O", s, L2), 5: lambda s: ("O", s, SA), 6: lambda s: ("O", s, CA)}
X_NORM = {L1: 0, L2: 2, SA: 4, CA: 5}
COLS = {}


def _columns():
    at = 0
    for name, n in (("b0q", 8), ("b0k", 8), ("b0v", 8), ("b0o", 2), ("g0", 2), ("be0", 2),
                    ("b1o", 2), ("g1", 2), ("be1", 2), ("b1f", 8), ("b1g", 2), ("g2", 2), ("be2", 2),
                    ("b2q", 2), ("b2k", 2), ("b2v", 2), ("b2o", 2), ("g3", 2), ("be3", 2),
                    ("b3q", 2), ("b3k", 2), ("b3v", 2), ("b3o", 2), ("b4q", 2), ("b4k", 2), ("b4v", 2),
                    ("b4o", 2), ("b5f", 8), ("b5g", 2),
                    ("g4", 2), ("be4", 2), ("g5", 2), ("be5", 2), ("g6", 2), ("be6", 2)):
        COLS[name] = (at, n)
        at += n
    return at


N_COLS = _columns()


def build(nc, t):
    with ExitStack() as ctx:
        def sb(name, shape, dt=F32):
            return ctx.enter_context(nc.sbuf_tensor(name, shape, dt))

        def ps(name, shape, dt=F32):
            return ctx.enter_context(nc.psum_tensor(name, shape, dt))

        class Signal:
            every = []

            def __init__(self, name, per_turn):
                self.sem = ctx.enter_context(nc.semaphore(name))
                self.per_turn = per_turn
                Signal.every.append(self)

            def at(self, turn, n):
                assert n + self.per_turn > 0, n
                return turn * self.per_turn + (self.per_turn + n)

        Signal.every = []

        def pair(name, per_turn):
            return [Signal(f"{name}_{i}", per_turn) for i in range(2)]

        w0q, w0k, w0v = (sb(n, [P, KT, 1024]) for n in ("w0q", "w0k", "w0v"))
        w0o = sb("w0o", [P, FT, D])
        w1q, w1k, w1v = (sb(n, [P, P]) for n in ("w1q", "w1k", "w1v"))
        w1o = sb("w1o", [P, KT, D])
        w1f, w1g = sb("w1f", [P, KT, 1024]), sb("w1g", [P, FT, D])
        w2q, w2k, w2v, w2o = (sb(n, [P, KT, D]) for n in ("w2q", "w2k", "w2v", "w2o"))
        w3q, w3k, w3v, w3o = (sb(n, [P, KT, D]) for n in ("w3q", "w3k", "w3v", "w3o"))
        w4q, w4k, w4v, w4o = (sb(n, [P, KT, D]) for n in ("w4q", "w4k", "w4v", "w4o"))
        w5f, w5g = sb("w5f", [P, KT, 1024]), sb("w5g", [P, FT, D])
        cols = sb("cols", [P, N_COLS])

        def col(name, i):
            return cols[:, COLS[name][0] + i:COLS[name][0] + i + 1]

        ident = sb("ident", [P, P])
        ident_b = sb("ident_b", [P, P], BF16)
        ident_r = sb("ident_r", [H, H], F32R)
        parity = sb("parity", [P, 2])
        few_rows = sb("few_rows", [P, 2, S], F32R)
        k_fixed = few_rows[0:32, :, :]
        q_fixed = few_rows[32:35, 0, :]
        pen1_row = [few_rows[64:65, s, :] for s in range(STREAMS)]
        mask1_row = [few_rows[96:97, s, :].bitcast(mybir.dt.int32) for s in range(STREAMS)]
        half = sb("half", [P, KT])
        pen3 = sb("pen3", [P, QT, S], BF16)
        pen3_t = sb("pen3_t", [P, QT, S], BF16)
        flag = sb("flag", [P, 4 * QT])

        two = range(STREAMS)
        q_st = [sb(f"q_st{s}", [P, PAIRS, S], F32R) for s in two]
        k_st = [sb(f"k_st{s}", [P, H, S], F32R) for s in two]
        inner = [sb(f"inner{s}", [P, FT, S]) for s in two]
        v_aug = [sb(f"v_aug{s}", [P, QT * H0 * SLOT0]) for s in two]
        rows = [sb(f"rows{s}", [P, QT, D]) for s in two]
        x_t = [sb(f"x_t{s}", [P, KT, S]) for s in two]
        y_t = [sb(f"y_t{s}", [P, KT, S]) for s in two]
        ctx_t = [sb(f"ctx_t{s}", [P, KT, S]) for s in two]
        mask0 = [sb(f"mask0{s}", [P, QT, S], mybir.dt.uint8) for s in two]
        pen0 = [sb(f"pen0{s}", [P, QT, S], BF16) for s in two]
        pen0_t = [sb(f"pen0_t{s}", [P, QT, S], BF16) for s in two]
        mask1_col = [sb(f"mask1_col{s}", [P, QT], mybir.dt.int32) for s in two]
        pen1_col = [sb(f"pen1_col{s}", [P, QT]) for s in two]
        neg_max = [sb(f"neg_max{s}", [P, QT, H]) for s in two]
        neg_max_t = [sb(f"neg_max_t{s}", [H, S], F32R) for s in two]
        stats = [sb(f"stats{s}", [P, QT, 6]) for s in two]
        mean_var = [sb(f"mean_var{s}", [P, QT, 2]) for s in two]
        var_eps = [sb(f"var_eps{s}", [P, QT]) for s in two]
        rstd = [sb(f"rstd{s}", [P, QT]) for s in two]

        fixed = inner[0][0:32, 0:3, :]

        def split(s, i):
            return inner[s][:, 2 * i:2 * i + 2, :].bitcast(F32R)

        Q_HI, Q_LO, K_HI, K_LO = range(4)

        def v0(s):
            return v_aug[s][:, :].rearrange("p (t h c) -> p t h c", t=QT, h=H0)

        def v16(s):
            return v_aug[s][:, 0:QT * H * SLOT].rearrange("p (t h c) -> p t h c", t=QT, h=H)

        def rows0(s, g):
            return rows[s][:, g % 2, :].rearrange("p (t c) -> p t c", t=QT)

        probs = [sb(f"probs{w}", [P, QT, 2, S]) for w in two]
        summed = [sb(f"summed{c}", [P, 2 * S]) for c in two]
        recip = [sb(f"recip{c}", [P, 2 * 4]) for c in two]

        wide = [ps(f"wide{w}", [P, QT, 2, S]) for w in two]
        acc = [ps(f"acc{c}", [P, 2 * S]) for c in two]
        misc = [ps(f"misc{b}", [P, 2, S]) for b in two]

        def flat(b):
            return misc[b][:, :, :].rearrange("p a b -> p (a b)")

        misc_full = pair("misc_full", N_USES // 2)
        misc_free = pair("misc_free", N_USES // 2)
        scores = pair("scores", N_UNITS // 2)
        exp_done = pair("exp_done", N_UNITS // 2)
        pv_done = pair("pv_done", N_UNITS // 2)
        summed_ready = pair("summed_ready", N_GROUPS // 2)
        recip_ready = pair("recip_ready", N_GROUPS // 2)
        bn_ready = Signal("bn_ready", N_NORMS)
        mv_ready = Signal("mv_ready", N_NORMS)
        eps_ready = Signal("eps_ready", N_NORMS)
        rstd_ready = Signal("rstd_ready", N_NORMS)
        kq_hi = pair("kq_hi", 16)
        q_dma = pair("q_dma", 16 * Q_DMAS * 4)
        k_dma = pair("k_dma", 16 * sum(K_DMAS.values()))
        fix_dma = pair("fix_dma", 16 * 2)
        k_masked = pair("k_masked", 4)
        k_zeroed = pair("k_zeroed", 2)
        m_dma = pair("m_dma", 16 * sum(M_DMAS.values()))
        ones_ready = pair("ones_ready", 2)
        pen_ready = pair("pen_ready", 3)
        load_x = pair("load_x", 16)
        load_ctx = pair("load_ctx", 16)
        load_mask = pair("load_mask", 16 * 3)
        out_dma = pair("out_dma", 16)
        primed = ctx.enter_context(nc.semaphore("primed"))
        settled = ctx.enter_context(nc.semaphore("settled"))
        w_dma = ctx.enter_context(nc.semaphore("w_dma"))
        const_ready = ctx.enter_context(nc.semaphore("const_ready"))
        flag_step = ctx.enter_context(nc.semaphore("flag_step"))
        pen3_in = ctx.enter_context(nc.semaphore("pen3_in"))
        pen3_turned = ctx.enter_context(nc.semaphore("pen3_turned"))
        bd_zeroed = ctx.enter_context(nc.semaphore("bd_zeroed"))

        N_CONST = 8
        weights = [(w0q, "w0q", KT), (w0k, "w0k", KT), (w0v, "w0v", KT), (w0o, "w0o", FT), (w1o, "w1o", KT),
                   (w1f, "w1f", KT), (w1g, "w1g", FT), (w2q, "w2q", KT), (w2k, "w2k", KT), (w2v, "w2v", KT),
                   (w2o, "w2o", KT), (w3q, "w3q", KT), (w3k, "w3k", KT), (w3v, "w3v", KT), (w3o, "w3o", KT),
                   (w4q, "w4q", KT), (w4k, "w4k", KT), (w4v, "w4v", KT), (w4o, "w4o", KT),
                   (w5f, "w5f", KT), (w5g, "w5g", FT)]
        N_W = 16 * (len(weights) + 5 + 3 * 8)
        mask3 = mask0[0]

        def last_unit(s, a):
            if a == L0A:
                return UNIT_NO[s, CA, units(CA) - 1] - N_UNITS
            return UNIT_NO[s, a - 1, units(a - 1) - 1]

        def wait_scores_read(eng, i, s, a):
            e = last_unit(s, a)
            eng.wait_ge(exp_done[e % 2].sem, exp_done[e % 2].at(i, e // 2 + 1))

        def wait_v_read(eng, i, s, a):
            e = last_unit(s, a)
            eng.wait_ge(pv_done[e % 2].sem, pv_done[e % 2].at(i, e // 2 + 1))

        def wait_misc_full(eng, i, u):
            eng.wait_ge(misc_full[u % 2].sem, misc_full[u % 2].at(i, u // 2 + 1))

        def wait_misc_free(eng, i, u):
            eng.wait_ge(misc_free[u % 2].sem, misc_free[u % 2].at(i, u // 2))

        def wait_result(eng, i, kind, s, a, n=0):
            u = LAST_USE[kind, s, a, n]
            eng.wait_ge(misc_free[u % 2].sem, misc_free[u % 2].at(i, u // 2 + 1))

        def settle(eng):
            eng.sem_inc(settled, 1)

        block = ctx.enter_context(nc.Block())

        @block.sync
        def _(sp):
            for tile, name, n in weights:
                sp.dma_start(tile[:, :, :], t[name].rearrange("(k p) n -> p k n", p=P)).then_inc(w_dma, 16)
            sp.dma_start(cols[:, :], t["cols"]).then_inc(w_dma, 16)
            sp.dma_start(ident[:, :], t["ident"]).then_inc(w_dma, 16)
            sp.dma_start(parity[:, :], t["parity"]).then_inc(w_dma, 16)
            sp.dma_start(fixed, t["fixed"]).then_inc(w_dma, 16)
            sp.dma_start(mask3[:, :, :], t["mask3"].rearrange("(t p) k -> p t k", p=P)).then_inc(w_dma, 16)
            sp.wait_ge(bd_zeroed, 3)
            for tile, name in ((w1q, "w1q"), (w1k, "w1k"), (w1v, "w1v")):
                for h in range(8):
                    sp.dma_start(tile[16 * h:16 * h + 16, 16 * h:16 * h + 16], t[name]).then_inc(w_dma, 16)
            sp.wait_ge(primed, 1)
            sp.wait_ge(flag_step, 3)
            sp.wait_ge(const_ready, N_CONST)

            with sp.Fori(0, TURNS) as i:
                for s in two:
                    b = i * STREAMS + s
                    sp.wait_ge(out_dma[s].sem, out_dma[s].at(i, 0))
                    settle(sp)
                    sp.dma_start(rows[s][:, :, :], t["ctx"][bass.ds(b, 1)].rearrange("b (t p) d -> p (b t) d", p=P)
                                 ).then_inc(load_ctx[s].sem, 16)
                    sp.dma_start(y_t[s][:, :, :], t["x"][bass.ds(b, 1)].rearrange("b (t p) d -> p (b t) d", p=P)
                                 ).then_inc(load_x[s].sem, 16)
                    sp.dma_start(mask0[s][:, :, :], t["mask0"][bass.ds(b, 1)].rearrange("b (t p) k -> p (b t) k", p=P)
                                 ).then_inc(load_mask[s].sem, 16)
                    sp.dma_start(mask1_row[s], t["mask1"][bass.ds(b, 1)]).then_inc(load_mask[s].sem, 16)
                    sp.dma_start(mask1_col[s][:, :], t["mask1_cols"][bass.ds(b, 1)].rearrange("b p t -> p (b t)")
                                 ).then_inc(load_mask[s].sem, 16)
                for st in STEPS:
                    s, a = st.s, st.a
                    if st.kind == "K":
                        wait_scores_read(sp, i, s, a)
                        settle(sp)
                        if a == L1:
                            for j in range(2):
                                sp.dma_start(k_st[s][96:128, j::2, :].bitcast(F32),
                                             k_fixed[:, j:j + 1, :].bitcast(F32).to_broadcast([32, PAIRS, S])
                                             ).then_inc(fix_dma[s].sem, 16)
                        wait_result(sp, i, "K", s, a)
                        for p4 in range(4):
                            r = slice(32 * p4, 32 * p4 + 32)
                            for term, part in enumerate((K_HI, K_HI, K_LO)):
                                sp.dma_start(k_st[s][32 * term:32 * term + 32, 2 * p4::8, :].bitcast(F32),
                                             split(s, part)[r].bitcast(F32)
                                             ).then_inc(k_dma[s].sem, 16)
                        if a == L1:
                            sp.wait_ge(fix_dma[s].sem, fix_dma[s].at(i, 32))
                            settle(sp)
                            sp.wait_ge(pen_ready[s].sem, pen_ready[s].at(i, 3))
                            sp.dma_start(k_st[s][98:99, :, :].bitcast(F32),
                                         pen1_row[s].bitcast(F32).unsqueeze(1).to_broadcast([1, H, S])
                                         ).then_inc(k_dma[s].sem, 16)
                    elif st.kind == "Q":
                        n = 3 if a == L1 else 2
                        sp.dma_start(q_st[s][96:96 + n, :, :].bitcast(F32),
                                     q_fixed[0:n, :].bitcast(F32).unsqueeze(1).to_broadcast([n, PAIRS, S])
                                     ).then_inc(q_dma[s].sem, 16)
                        wait_result(sp, i, "Q", s, a)
                        for p4 in range(4):
                            r = slice(32 * p4, 32 * p4 + 32)
                            for term, part in enumerate((Q_HI, Q_LO, Q_HI)):
                                sp.dma_start(q_st[s][32 * term:32 * term + 32, p4::4, :].bitcast(F32),
                                             split(s, part)[r].bitcast(F32)
                                             ).then_inc(q_dma[s].sem, 16)
                    elif st.kind == "MT" and a >= L1:
                        wait_result(sp, i, "MT", s, a)
                        for j in range(2):
                            sp.dma_start(q_st[s][96 + j:97 + j, :, :].bitcast(F32),
                                         neg_max_t[s][8 * j:8 * j + 8, :].bitcast(F32)
                                         ).then_inc(m_dma[s].sem, 16)
                        if a == L1:
                            sp.dma_start(k_st[s][98:99, :, :].bitcast(F32),
                                         q_fixed[0:1, :].bitcast(F32).unsqueeze(1).to_broadcast([1, H, S])
                                         ).then_inc(m_dma[s].sem, 16)
                    elif st.kind == "OUT":
                        b = i * STREAMS + s
                        wait_result(sp, i, "OUT", s, a)
                        settle(sp)
                        sp.dma_start(t["out"][bass.ds(b, 1)].rearrange("b (t p) d -> p (b t) d", p=P), rows[s][:, :, :]
                                     ).then_inc(out_dma[s].sem, 16)
            for s in two:
                sp.wait_ge(out_dma[s].sem, out_dma[s].per_turn * (TURNS + 1))

        @block.gpsimd
        def _(pool):
            for sig in Signal.every:
                pool.sem_inc(sig.sem, sig.per_turn)
            pool.sem_inc(primed, 1)
            for tile in (w1q, w1k, w1v):
                nc.gpsimd.memset(tile[:, :], 0.0).then_inc(bd_zeroed, 1)
            nc.gpsimd.memset(half[:, :], -0.5).then_inc(const_ready, 1)
            for s in two:
                nc.gpsimd.memset(neg_max[s][:, :, :], 0.0).then_inc(const_ready, 1)
                nc.gpsimd.memset(v_aug[s][:, :], 0.0).then_inc(const_ready, 1)
            pool.wait_ge(const_ready, N_CONST)

            with pool.Fori(0, TURNS) as i:
                for st in STEPS:
                    s, a = st.s, st.a
                    if st.kind == "K0" and a == L0A:
                        wait_scores_read(pool, i, s, a)
                        settle(pool)
                        if s == 0:
                            pool.wait_ge(rstd_ready.sem, rstd_ready.at(i, 0))
                        else:
                            pool.wait_ge(ones_ready[0].sem, ones_ready[0].at(i, 1))
                        settle(pool)
                        nc.gpsimd.memset(k_st[s][64:128, 0::2, :].bitcast(F32), 0.0).then_inc(k_zeroed[s].sem, 1)
                        pool.wait_ge(k_zeroed[s].sem, k_zeroed[s].at(i, 1))
                        settle(pool)
                        nc.gpsimd.memset(k_st[s][0:64, 1::2, :].bitcast(F32), 0.0).then_inc(k_zeroed[s].sem, 1)
                    elif st.kind == "V0" and a == L0A:
                        wait_v_read(pool, i, s, a)
                        pool.wait_ge(k_zeroed[s].sem, k_zeroed[s].at(i, 2))
                        settle(pool)
                        nc.gpsimd.memset(v0(s)[:, :, :, 64:66], 1.0).then_inc(ones_ready[s].sem, 1)
                    elif st.kind == "V" and a == L1:
                        wait_v_read(pool, i, s, a)
                        settle(pool)
                        nc.gpsimd.memset(v16(s)[:, :, :, 16:17], 1.0).then_inc(ones_ready[s].sem, 1)
                    elif st.kind == "LNa":
                        pool.wait_ge(mv_ready.sem, mv_ready.at(i, st.l + 1))
                        settle(pool)
                        nc.gpsimd.tensor_scalar(var_eps[s][:, :], mean_var[s][:, :, 1], EPS, None, ALU.add
                                                ).then_inc(eps_ready.sem, 1)
                        pool.wait_ge(eps_ready.sem, eps_ready.at(i, st.l + 1))
                        settle(pool)
                        nc.gpsimd.tensor_tensor(rstd[s][:, :], var_eps[s][:, :], half[:, :], ALU.pow
                                                ).then_inc(rstd_ready.sem, 1)

        @block.tensor
        def _(pe):
            mm = nc.tensor.matmul
            turn = nc.tensor.transpose
            pe.wait_ge(primed, 1)
            pe.wait_ge(w_dma, N_W)
            pe.wait_ge(const_ready, N_CONST)
            pe.wait_ge(pen3_in, 1)
            for kt in range(QT):
                for qt in range(QT):
                    ins = turn(flat(0).bitcast(BF16)[:, kt * S + qt * P:kt * S + qt * P + P],
                               pen3[:, qt, kt * P:kt * P + P], ident_b[:, :])
            ins.then_inc(pen3_turned, 1)
            pe.wait_ge(pen3_turned, 2)

            def project(b, w, x, tiles):
                for half_, m in enumerate(tiles):
                    n = w.shape[1]
                    for k in range(n):
                        ins = mm(misc[b][:, half_, :], w[:, k, m * P:m * P + P], x[:, k, :],
                                 start=k == 0, stop=k == n - 1)
                return ins

            def turn_square(b, src):
                for i_ in range(2):
                    for j_ in range(2):
                        ins = turn(misc[b][:, j_, i_ * P:i_ * P + P], src[:, i_, j_ * P:j_ * P + P], ident[:, :])
                return ins

            def product_with_v(i, s, a, n):
                e = UNIT_NO[s, a, n]
                w = e % 2
                g = GROUP_NO[s, a, n if a < L1 else n // 2]
                pe.wait_ge(exp_done[w].sem, exp_done[w].at(i, e // 2 + 1))
                if n == 0:
                    wait_result(pe, i, "V0" if a < L1 else "V", s, a)
                    pe.wait_ge(ones_ready[s].sem, ones_ready[s].at(i, 1 if a < L1 else 2))
                if a < L1 or n % 2 == 0:
                    pe.wait_ge(summed_ready[g % 2].sem, summed_ready[g % 2].at(i, g // 2))
                for j in range(2):
                    for kt in range(QT):
                        if a < L1:
                            out, v = acc[g % 2][0:SLOT0, j * S:j * S + S], v0(s)[:, kt, 2 * n + j, :]
                        else:
                            r = SLOT * ((2 * n + j) % 4)
                            out, v = acc[g % 2][r:r + SLOT, 0:S], v16(s)[:, kt, 2 * n + j, :]
                        ins = mm(out, v, probs[w][:, kt, j, :], start=kt == 0, stop=kt == QT - 1)
                ins.then_inc(pv_done[w].sem, 1)

            with pe.Fori(0, TURNS) as i:
                for st in STEPS:
                    s, a, n, u = st.s, st.a, st.n, st.u
                    b = u % 2
                    kind = st.kind
                    if kind in ("E", "EL"):
                        if kind == "E":
                            w = st.e % 2
                            if n == 0:
                                wait_result(pe, i, "MT", s, a)
                                if a >= L1:
                                    total = 16 * sum(M_DMAS[x] for x in range(L1, a + 1))
                                    pe.wait_ge(m_dma[s].sem, m_dma[s].at(i, total))
                            pe.wait_ge(exp_done[w].sem, exp_done[w].at(i, st.e // 2))
                            pen = {L0A: pen0_t[s], L0B: pen0_t[s], SA: pen3_t}.get(a)
                            for kt in range(QT):
                                keys = slice(kt * P, kt * P + P)
                                if pen is not None:
                                    ins = mm(wide[w][:, kt, :, :], ident_b[:, :],
                                             pen[:, kt:kt + 1, :].to_broadcast([P, 2, S]),
                                             start=True, stop=False, skip_group_check=True)
                                for j in range(2):
                                    out = wide[w][:, kt, j, :]
                                    first = pen is None and j == 0
                                    if a < L1:
                                        for kk, qq in ((2 * n + j, n), (2 * n + j, 4 + n), (8 + 2 * n + j, n)):
                                            mm(out, k_st[s][:, kk, keys], q_st[s][:, qq, :],
                                               start=False, stop=False, skip_group_check=True)
                                        r = 8 * j + n
                                        ins = mm(out, ident_r[:, r:r + 1].to_broadcast([H, P]), neg_max_t[s][:, :],
                                                 start=False, stop=True, skip_group_check=True)
                                    else:
                                        ins = mm(out, k_st[s][:, 2 * n + j, keys], q_st[s][:, n, :],
                                                 start=first, stop=True, skip_group_check=True)
                            ins.then_inc(scores[w].sem, 1)
                        if n >= 1:
                            product_with_v(i, s, a, n - 1)
                        continue
                    wait_misc_free(pe, i, u)
                    if kind == "CT":
                        pe.wait_ge(load_ctx[s].sem, load_ctx[s].at(i, 16))
                        ins = turn_square(b, rows[s])
                    elif kind == "XT":
                        pe.wait_ge(load_x[s].sem, load_x[s].at(i, 16))
                        ins = turn_square(b, y_t[s])
                    elif kind == "PEN":
                        pe.wait_ge(pen_ready[s].sem, pen_ready[s].at(i, 1))
                        for kt in range(QT):
                            for qt in range(QT):
                                ins = turn(flat(b).bitcast(BF16)[:, kt * S + qt * P:kt * S + qt * P + P],
                                           pen0[s][:, qt, kt * P:kt * P + P], ident_b[:, :])
                    elif kind in ("K0", "Q0"):
                        if kind == "K0":
                            wait_result(pe, i, "CT", s, L0A)
                        else:
                            wait_result(pe, i, "XT", s, L0A)
                        for r in range(2):
                            if r:
                                ins.then_inc(misc_full[b].sem, 1)
                                b = (u + 1) % 2
                                wait_misc_free(pe, i, u + 1)
                            t0 = 4 * a + 2 * r
                            ins = project(b, w0k if kind == "K0" else w0q, ctx_t[s] if kind == "K0" else x_t[s],
                                          (t0, t0 + 1))
                    elif kind == "V0":
                        for tt in range(QT):
                            if tt:
                                ins.then_inc(misc_full[b].sem, 1)
                                b = (u + 1) % 2
                                wait_misc_free(pe, i, u + 1)
                            for k in range(KT):
                                ins = mm(flat(b), ctx_t[s][:, k, tt * P:tt * P + P], w0v[:, k, 512 * a:512 * a + 512],
                                         start=k == 0, stop=k == KT - 1)
                    elif kind in ("K", "Q"):
                        if kind == "Q" or a == SA:
                            wait_result(pe, i, "LNb", s, X_NORM[a])
                        x = x_t[s] if kind == "Q" or a == SA else ctx_t[s]
                        if a == L1:
                            for m in range(KT):
                                ins = mm(misc[b][:, m, :], (w1q if kind == "Q" else w1k)[:, :], x[:, m, :],
                                         start=True, stop=True)
                        else:
                            w = {"Q": {L2: w2q, SA: w3q, CA: w4q}, "K": {L2: w2k, SA: w3k, CA: w4k}}[kind][a]
                            ins = project(b, w, x, (0, 1))
                    elif kind == "V":
                        x = x_t[s] if a == SA else ctx_t[s]
                        for tt in range(QT):
                            tok = slice(tt * P, tt * P + P)
                            if a == L1:
                                for k in range(KT):
                                    ins = mm(misc[b][:, tt, k * P:k * P + P], x[:, k, tok], w1v[:, :],
                                             start=True, stop=True)
                            else:
                                w = {L2: w2v, SA: w3v, CA: w4v}[a]
                                for k in range(KT):
                                    ins = mm(misc[b][:, tt, :], x[:, k, tok], w[:, k, :], start=k == 0, stop=k == KT - 1)
                    elif kind == "X":
                        pairs = units(a)
                        qt, p = n // pairs, n % pairs
                        if n == 0:
                            if a < L1:
                                wait_result(pe, i, "Q0", s, a)
                                pe.wait_ge(k_zeroed[s].sem, k_zeroed[s].at(i, 2))
                            else:
                                pe.wait_ge(q_dma[s].sem, q_dma[s].at(i, 16 * Q_DMAS * (a - L1 + 1)))
                                pe.wait_ge(k_masked[s].sem, k_masked[s].at(i, a - L1 + 1))
                        rows_q = slice(qt * P, qt * P + P)
                        pen = {L0A: pen0[s], L0B: pen0[s], SA: pen3}.get(a)
                        if pen is not None:
                            mm(misc[b][:, :, :], ident_b[:, :], pen[:, qt:qt + 1, :].to_broadcast([P, 2, S]),
                               start=True, stop=False)
                        if a < L1:
                            for qq, kk in ((p, 2 * p), (4 + p, 2 * p), (p, 8 + 2 * p)):
                                ins = mm(misc[b][:, :, :], q_st[s][:, qq, rows_q], k_st[s][:, kk:kk + 2, :],
                                         start=False, stop=kk >= 8)
                        else:
                            ins = mm(misc[b][:, :, :], q_st[s][:, p, rows_q], k_st[s][:, 2 * p:2 * p + 2, :],
                                     start=pen is None, stop=True)
                    elif kind == "MT":
                        wait_result(pe, i, "X", s, a, QT * units(a) - 1)
                        for qt in range(QT):
                            ins = turn(misc[b][0:H, 0, qt * P:qt * P + P], neg_max[s][:, qt, :], ident[:, :])
                    elif kind == "N":
                        g = st.g
                        pe.wait_ge(summed_ready[g % 2].sem, summed_ready[g % 2].at(i, g // 2 + 1))
                        for qt in range(QT):
                            if a < L1:
                                for j in range(2):
                                    at = SLOT0 * (2 * qt + j)
                                    ins = turn(flat(b)[:, at:at + SLOT0],
                                               summed[g % 2][0:SLOT0, j * S + qt * P:j * S + qt * P + P],
                                               ident[0:SLOT0, 0:SLOT0])
                            else:
                                ins = turn(misc[b][:, 0, qt * P:qt * P + P], summed[g % 2][:, qt * P:qt * P + P],
                                           ident[:, :])
                    elif kind == "T0":
                        wait_result(pe, i, "N", s, a, n)
                        for qt in range(QT):
                            ins = turn(misc[b][:, 0, qt * P:qt * P + P], rows0(s, n)[:, qt, :], ident[:, :])
                    elif kind == "T":
                        wait_result(pe, i, "N", s, a, 3)
                        ins = turn_square(b, rows[s])
                    elif kind == "O":
                        wait_result(pe, i, *(("T0", s, a, 3) if a < L1 else ("T", s, a)))
                        w = {L0B: w0o, L1: w1o, L2: w2o, SA: w3o, CA: w4o}[a]
                        ins = project(b, w, inner[s], (0, 1))
                    elif kind == "LNa":
                        if a == 4:
                            wait_result(pe, i, "LNb", s, 3)
                        else:
                            wait_result(pe, i, *SUMMED_BY[a](s))
                        ins = turn_square(b, y_t[s])
                    elif kind == "LNb":
                        wait_result(pe, i, "LNa", s, a)
                        ins = turn_square(b, rows[s])
                    elif kind == "F1":
                        if n == 0:
                            wait_result(pe, i, "LNb", s, a)
                        ins = project(b, w1f if a == 1 else w5f, x_t[s], (2 * n, 2 * n + 1))
                    elif kind == "F2":
                        wait_result(pe, i, "F1", s, a, 2)
                        wait_result(pe, i, "F1", s, a, 3)
                        ins = project(b, w1g if a == 1 else w5g, inner[s], (0, 1))
                    elif kind == "OUT":
                        wait_result(pe, i, "F2", s, 6)
                        ins = turn_square(b, y_t[s])
                    ins.then_inc(misc_full[b].sem, 1)

        @block.scalar
        def _(act):
            fn = nc.scalar.activation
            act.wait_ge(primed, 1)
            act.wait_ge(w_dma, N_W)
            act.wait_ge(const_ready, N_CONST)
            act.wait_ge(flag_step, 3)

            with act.Fori(0, TURNS) as i:
                for st in STEPS:
                    s, a, n, u = st.s, st.a, st.n, st.u
                    b = u % 2
                    kind = st.kind
                    if kind == "E":
                        w = st.e % 2
                        act.wait_ge(scores[w].sem, scores[w].at(i, st.e // 2 + 1))
                        act.wait_ge(pv_done[w].sem, pv_done[w].at(i, st.e // 2))
                        if a == L1:
                            for kt in range(QT):
                                ins = fn(probs[w][:, kt, :, :], wide[w][:, kt, :, :], ACT.Exp,
                                         bias=pen1_col[s][:, kt:kt + 1], scale=SCALE[a])
                        else:
                            ins = fn(probs[w][:, :, :, :], wide[w][:, :, :, :], ACT.Exp, scale=SCALE[a])
                        ins.then_inc(exp_done[w].sem, 1)
                    elif kind == "N":
                        g = st.g
                        e = UNIT_NO[s, a, n if a < L1 else 2 * n + 1]
                        act.wait_ge(pv_done[e % 2].sem, pv_done[e % 2].at(i, e // 2 + 1))
                        if a < L1:
                            ins = nc.scalar.copy(summed[g % 2][0:SLOT0, :], acc[g % 2][0:SLOT0, :])
                        else:
                            ins = nc.scalar.copy(summed[g % 2][:, 0:S], acc[g % 2][:, 0:S])
                        ins.then_inc(summed_ready[g % 2].sem, 1)
                    elif kind in ("CT", "XT"):
                        wait_misc_full(act, i, u)
                        dst = ctx_t[s] if kind == "CT" else x_t[s]
                        nc.scalar.copy(dst[:, :, :], misc[b][:, :, :]).then_inc(misc_free[b].sem, 1)
                    elif kind == "K0":
                        wait_scores_read(act, i, s, a)
                        for r in range(2):
                            b = (u + r) % 2
                            wait_misc_full(act, i, u + r)
                            for half_ in range(2):
                                tile = 2 * r + half_
                                for j in range(2):
                                    rr = slice(64 * j, 64 * j + 64)
                                    c = COLS["b0k"][0] + 4 * a + tile
                                    ins = fn(k_st[s][rr, 2 * tile + j, :], misc[b][rr, half_, :], ACT.Identity,
                                             bias=cols[rr, c:c + 1])
                            ins.then_inc(kq_hi[s].sem, 1)
                    elif kind == "Q0":
                        for r in range(2):
                            b = (u + r) % 2
                            wait_misc_full(act, i, u + r)
                            for half_ in range(2):
                                tile = 2 * r + half_
                                ins = fn(q_st[s][:, tile, :], misc[b][:, half_, :], ACT.Identity,
                                         bias=col("b0q", 4 * a + tile))
                            ins.then_inc(kq_hi[s].sem, 1)
                    elif kind in ("K", "Q"):
                        wait_misc_full(act, i, u)
                        part = split(s, K_HI if kind == "K" else Q_HI)
                        for m in range(KT):
                            if a == L1:
                                ins = nc.scalar.activation(part[:, m, :], misc[b][:, m, :], ACT.Identity)
                            else:
                                name = {L2: "b2", SA: "b3", CA: "b4"}[a] + kind.lower()
                                ins = fn(part[:, m, :], misc[b][:, m, :], ACT.Identity, bias=col(name, m))
                        ins.then_inc(kq_hi[s].sem, 1)
                    elif kind == "V0":
                        wait_v_read(act, i, s, a)
                        for tt in range(QT):
                            b = (u + tt) % 2
                            wait_misc_full(act, i, u + tt)
                            nc.scalar.copy(v0(s)[:, tt, :, 0:64], flat(b).rearrange("p (h c) -> p h c", h=H0)
                                           ).then_inc(misc_free[b].sem, 1)
                    elif kind == "V":
                        wait_v_read(act, i, s, a)
                        wait_misc_full(act, i, u)
                        nc.scalar.copy(v16(s)[:, :, :, 0:16], misc[b][:, :, :].rearrange("p t (h c) -> p t h c", h=H)
                                       ).then_inc(misc_free[b].sem, 1)
                    elif kind == "MT":
                        wait_misc_full(act, i, u)
                        nc.scalar.copy(neg_max_t[s][:, :], misc[b][0:H, 0, :]).then_inc(misc_free[b].sem, 1)
                    elif kind == "T0":
                        wait_misc_full(act, i, u)
                        fn(inner[s][:, 4 * a + n, :], misc[b][:, 0, :], ACT.Identity, bias=col("b0v", 4 * a + n)
                           ).then_inc(misc_free[b].sem, 1)
                    elif kind == "T":
                        wait_misc_full(act, i, u)
                        for m in range(KT):
                            if a == L1:
                                ins = nc.scalar.activation(inner[s][:, m, :], misc[b][:, m, :], ACT.Identity)
                            else:
                                ins = fn(inner[s][:, m, :], misc[b][:, m, :], ACT.Identity,
                                         bias=col({L2: "b2v", SA: "b3v", CA: "b4v"}[a], m))
                        ins.then_inc(misc_free[b].sem, 1)
                    elif kind == "LNb":
                        wait_misc_full(act, i, u)
                        dst = y_t[s] if a == 3 else x_t[s]
                        for m in range(KT):
                            ins = fn(dst[:, m, :], misc[b][:, m, :], ACT.Identity, bias=col(f"be{a}", m),
                                     scale=col(f"g{a}", m))
                        ins.then_inc(misc_free[b].sem, 1)
                    elif kind == "F1" and n % 2 == 0:
                        wait_misc_full(act, i, u)
                        for half_ in range(2):
                            m = 2 * n + half_
                            ins = fn(inner[s][:, m, :], misc[b][:, half_, :], ACT.Relu,
                                     bias=col("b1f" if a == 1 else "b5f", m))
                        ins.then_inc(misc_free[b].sem, 1)
                    elif kind == "OUT":
                        wait_misc_full(act, i, u)
                        for tt in range(QT):
                            ins = fn(rows[s][:, tt, :], misc[b][:, tt, :], ACT.Identity, bias=flag[:, 4 + tt:5 + tt])
                        ins.then_inc(misc_free[b].sem, 1)

        @block.vector
        def _(dve):
            v = nc.vector
            dve.wait_ge(primed, 1)
            dve.wait_ge(w_dma, N_W)
            v.tensor_copy(ident_b[:, :], ident[:, :]).then_inc(const_ready, 1)
            v.tensor_copy(ident_r[:, :], ident[0:H, 0:H])
            v.tensor_copy(k_fixed, fixed[:, 0:2, :]).then_inc(const_ready, 1)
            v.tensor_copy(q_fixed, fixed[0:3, 2, :]).then_inc(const_ready, 1)
            v.tensor_scalar(pen3[:, :, :], mask3[:, :, :], BIG, -BIG, ALU.mult, ALU.add).then_inc(pen3_in, 1)
            v.tensor_reduce(flag[:, 0:2], mask3[:, :, :], AX_X, ALU.max).then_inc(flag_step, 1)
            dve.wait_ge(flag_step, 1)
            v.reciprocal(flag[:, 2:4], flag[:, 0:2]).then_inc(flag_step, 1)
            dve.wait_ge(flag_step, 2)
            v.tensor_scalar(flag[:, 4:6], flag[:, 2:4], 0.0, None, ALU.mult).then_inc(flag_step, 1)
            dve.wait_ge(pen3_turned, 1)
            v.tensor_copy(pen3_t[:, :, :].rearrange("p t q -> p (t q)"), flat(0).bitcast(BF16)[:, 0:QT * S]
                          ).then_inc(pen3_turned, 1)
            dve.wait_ge(const_ready, N_CONST)

            with dve.Fori(0, TURNS) as i:
                for st in STEPS:
                    s, a, n, u = st.s, st.a, st.n, st.u
                    b = u % 2
                    kind = st.kind
                    if kind == "PEN":
                        dve.wait_ge(load_mask[s].sem, load_mask[s].at(i, 16 * 3))
                        v.tensor_scalar(pen0[s][:, :, :], mask0[s][:, :, :], -BIG, None, ALU.mult
                                        ).then_inc(pen_ready[s].sem, 1)
                        v.tensor_scalar(pen1_row[s], mask1_row[s], 0.0, -BIG, ALU.is_equal, ALU.mult
                                        ).then_inc(pen_ready[s].sem, 1)
                        v.tensor_scalar(pen1_col[s][:, :], mask1_col[s][:, :], 0.0, -BIG * SCALE[L1], ALU.is_equal, ALU.mult
                                        ).then_inc(pen_ready[s].sem, 1)
                        wait_misc_full(dve, i, u)
                        v.tensor_copy(pen0_t[s][:, :, :].rearrange("p t q -> p (t q)"), flat(b).bitcast(BF16)[:, 0:QT * S]
                                      ).then_inc(misc_free[b].sem, 1)
                    elif kind in ("K0", "Q0"):
                        for r in range(2):
                            b = (u + r) % 2
                            no = KQ_OPS[a] + (0 if kind == "K0" else 2) + r + 1
                            dve.wait_ge(kq_hi[s].sem, kq_hi[s].at(i, no))
                            for half_ in range(2):
                                tile = 2 * r + half_
                                if kind == "K0":
                                    for j in range(2):
                                        rr = slice(64 * j, 64 * j + 64)
                                        c = COLS["b0k"][0] + 4 * a + tile
                                        ins = v.scalar_tensor_tensor(
                                            k_st[s][rr, 8 + 2 * tile + j, :], misc[b][rr, half_, :], cols[rr, c:c + 1],
                                            k_st[s][rr, 2 * tile + j, :].bitcast(F32), ALU.add, ALU.subtract)
                                else:
                                    ins = v.scalar_tensor_tensor(
                                        q_st[s][:, 4 + tile, :], misc[b][:, half_, :], col("b0q", 4 * a + tile),
                                        q_st[s][:, tile, :].bitcast(F32), ALU.add, ALU.subtract)
                            ins.then_inc(misc_free[b].sem, 1)
                    elif kind in ("K", "Q"):
                        no = KQ_OPS[a] + (1 if kind == "K" else 2)
                        dve.wait_ge(kq_hi[s].sem, kq_hi[s].at(i, no))
                        hi, lo = (K_HI, K_LO) if kind == "K" else (Q_HI, Q_LO)
                        for m in range(KT):
                            hi_m = split(s, hi)[:, m, :].bitcast(F32)
                            if a == L1:
                                ins = v.tensor_tensor(split(s, lo)[:, m, :], misc[b][:, m, :], hi_m, ALU.subtract)
                            else:
                                name = {L2: "b2", SA: "b3", CA: "b4"}[a] + kind.lower()
                                ins = v.scalar_tensor_tensor(split(s, lo)[:, m, :], misc[b][:, m, :], col(name, m),
                                                             hi_m, ALU.add, ALU.subtract)
                        ins.then_inc(misc_free[b].sem, 1)
                    elif kind == "X":
                        pairs = units(a)
                        qt, p = n // pairs, n % pairs
                        if n == 0 and a >= L1:
                            total = 16 * sum(K_DMAS[x] for x in range(L1, a + 1))
                            dve.wait_ge(k_dma[s].sem, k_dma[s].at(i, total))
                            both = k_st[s][0:96, 0::2, :]
                            v.tensor_scalar(k_st[s][0:96, 1::2, :], both.bitcast(F32), parity[0:96, 1:2], None, ALU.mult)
                            v.tensor_scalar(both, both.bitcast(F32), parity[0:96, 0:1], None, ALU.mult
                                            ).then_inc(k_masked[s].sem, 1)
                        wait_misc_full(dve, i, u)
                        ins = v.tensor_reduce(neg_max[s][:, qt, p:p + 9:8], misc[b][:, :, :], AX_X, ALU.max, negate=True)
                        ins.then_inc(misc_free[b].sem, 1)
                    elif kind == "N":
                        g = st.g
                        wait_misc_full(dve, i, u)
                        if a < L1:
                            src = flat(b)[:, 0:4 * SLOT0].rearrange("p (m c) -> p m c", m=4)
                            m, width = 4, 64
                            dst = rows0(s, n).rearrange("p t (j c) -> p (t j) c", j=2)
                        else:
                            src = flat(b)[:, 0:S].rearrange("p (m c) -> p m c", c=SLOT)
                            m, width = 8, 16
                            dst = rows[s][:, :, 64 * n:64 * n + 64].rearrange("p t (j c) -> p t j c", j=4)
                        v.reciprocal(recip[g % 2][:, 0:m], src[:, :, width]).then_inc(recip_ready[g % 2].sem, 1)
                        dve.wait_ge(recip_ready[g % 2].sem, recip_ready[g % 2].at(i, g // 2 + 1))
                        if a < L1:
                            ins = v.tensor_tensor(dst, src[:, :, 0:width],
                                                  recip[g % 2][:, 0:m].unsqueeze(2).to_broadcast([P, m, width]), ALU.mult)
                        else:
                            src4 = flat(b)[:, 0:S].rearrange("p (t j c) -> p t j c", t=2, c=SLOT)
                            r4 = recip[g % 2][:, 0:8].rearrange("p (t j) -> p t j", t=2).unsqueeze(3)
                            ins = v.tensor_tensor(dst, src4[:, :, :, 0:16], r4.to_broadcast([P, 2, 4, 16]), ALU.mult)
                        ins.then_inc(misc_free[b].sem, 1)
                    elif kind in ("O", "F2"):
                        wait_misc_full(dve, i, u)
                        if kind == "F2":
                            bias, res, no = ("b1g", x_t, 3) if a == 1 else ("b5g", y_t, 7)
                        else:
                            bias = {L0B: "b0o", L1: "b1o", L2: "b2o", SA: "b3o", CA: "b4o"}[a]
                            res = y_t if a >= SA else x_t
                            no = {L0B: 1, L1: 2, L2: 4, SA: 5, CA: 6}[a]
                        for m in range(KT):
                            ins = v.scalar_tensor_tensor(y_t[s][:, m, :], misc[b][:, m, :], col(bias, m), res[s][:, m, :],
                                                         ALU.add, ALU.add)
                        ins.then_inc(misc_free[b].sem, 1)
                    elif kind == "LNa":
                        wait_misc_full(dve, i, u)
                        for tt in range(QT):
                            ins = v.bn_stats(stats[s][:, tt, :], misc[b][:, tt, :])
                        ins.then_inc(bn_ready.sem, 1)
                        dve.wait_ge(bn_ready.sem, bn_ready.at(i, st.l + 1))
                        settle(dve)
                        for tt in range(QT):
                            ins = v.bn_aggr(mean_var[s][:, tt, :], stats[s][:, tt, :])
                        ins.then_inc(mv_ready.sem, 1)
                        dve.wait_ge(rstd_ready.sem, rstd_ready.at(i, st.l + 1))
                        for tt in range(QT):
                            ins = v.tensor_scalar(rows[s][:, tt, :], misc[b][:, tt, :], mean_var[s][:, tt, 0:1],
                                                  rstd[s][:, tt:tt + 1], ALU.subtract, ALU.mult)
                        ins.then_inc(misc_free[b].sem, 1)
                    elif kind == "F1" and n % 2:
                        wait_misc_full(dve, i, u)
                        for half_ in range(2):
                            m = 2 * n + half_
                            ins = v.tensor_scalar(inner[s][:, m, :], misc[b][:, half_, :],
                                                  col("b1f" if a == 1 else "b5f", m), 0.0, ALU.add, ALU.max)
                        ins.then_inc(misc_free[b].sem, 1)


def shape_constants():
    ident = np.eye(P, dtype=np.float32)
    parity = np.zeros((P, 2), np.float32)
    for r in range(96):
        parity[r, (r % 32) // 16] = 1.0
    fixed = np.zeros((32, 3, S), np.float32)
    fixed[0, 0], fixed[1, 1] = 1.0, 1.0
    fixed[2, 2] = 1.0
    return {"ident": ident, "parity": parity, "fixed": fixed}


def kernel(**inputs):
    import concourse.bacc as bacc
    from concourse.bass_utils import run_bass_kernel_spmd

    a = {n: np.asarray(v) for n, v in inputs.items()}
    l0, l1, l2, l3 = (lambda n, k=k: a[f"L{k}_xattn_{n}"] for k in range(4))
    w2 = l2("W_qkv")
    arrays = {
        "x": a["x"], "ctx": a["ctx_1024"],
        "mask0": a["mask_BxSxS2_bf0"],
        "mask1": a["mask_Bx1x1xS2_if1"].reshape(B, S),
        "mask1_cols": a["mask_Bx1x1xS2_if1"].reshape(B, QT, P).transpose(0, 2, 1),
        "mask3": a["mask_1x1xSxS_bk0"].reshape(S, S),
        "w0q": l0("Wq"), "w0k": l0("Wk"), "w0v": l0("Wv"), "w0o": l0("Wo"),
        "w1q": l1("wq"), "w1k": l1("wk"), "w1v": l1("wv"), "w1o": l1("w_out"),
        "w1f": l1("w_ff1"), "w1g": l1("w_ff2"),
        "w2q": w2[0:D].T, "w2k": w2[D:2 * D].T, "w2v": w2[2 * D:].T, "w2o": l2("W_o").T,
        "w3q": l3("sa_wq"), "w3k": l3("sa_wk"), "w3v": l3("sa_wv"), "w3o": l3("sa_wo"),
        "w4q": l3("ca_wq"), "w4k": l3("ca_wk"), "w4v": l3("ca_wv"), "w4o": l3("ca_wo"),
        "w5f": l3("ff_w1"), "w5g": l3("ff_w2"),
    }
    b2 = l2("b_qkv")
    vectors = {
        "b0q": l0("bq"), "b0k": l0("bk"), "b0v": l0("bv"), "b0o": l0("bo"), "g0": l0("gamma"), "be0": l0("beta"),
        "b1o": l1("b_out"), "g1": l1("g1"), "be1": l1("beta1"), "b1f": l1("b_ff1"), "b1g": l1("b_ff2"),
        "g2": l1("g2"), "be2": l1("beta2"),
        "b2q": b2[0:D], "b2k": b2[D:2 * D], "b2v": b2[2 * D:], "b2o": l2("b_o"),
        "g3": l2("ln_gamma"), "be3": l2("ln_beta"),
        "b3q": l3("sa_bq"), "b3k": l3("sa_bk"), "b3v": l3("sa_bv"), "b3o": l3("sa_bo"),
        "b4q": l3("ca_bq"), "b4k": l3("ca_bk"), "b4v": l3("ca_bv"), "b4o": l3("ca_bo"),
        "b5f": l3("ff_b1"), "b5g": l3("ff_b2"),
        "g4": l3("ln1_g"), "be4": l3("ln1_b"), "g5": l3("ln2_g"), "be5": l3("ln2_b"),
        "g6": l3("ln3_g"), "be6": l3("ln3_b"),
    }
    arrays["cols"] = np.concatenate([vectors[n].reshape(-1, P).T for n in COLS], axis=1)
    arrays.update(shape_constants())
    arrays = {n: np.ascontiguousarray(v) for n, v in arrays.items()}

    nc = bacc.Bacc("TRN2", target_bir_lowering=False, num_devices=1)
    t = {n: nc.dram_tensor(f"in_{n}", v.shape, mybir.dt.from_np(v.dtype), kind="ExternalInput").ap()
         for n, v in arrays.items()}
    t["out"] = nc.dram_tensor("out", (B, S, D), F32, kind="ExternalOutput").ap()
    build(nc, t)
    r = run_bass_kernel_spmd(nc, [{f"in_{n}": v for n, v in arrays.items()}], core_ids=[0])
    return r.results[0]["out"]
```

```python
from contextlib import ExitStack
from collections import namedtuple

import numpy as np
import concourse.bass as bass
from concourse import mybir

F32 = mybir.dt.float32
F32R = mybir.dt.float32r
BF16 = mybir.dt.bfloat16
ALU = mybir.AluOpType
ACT = mybir.ActivationFunctionType
AX_X = mybir.AxisListType.X

P = 128
B, S, D = 32, 256, 256
KT = D // P
QT = S // P
STREAMS = 2
BANKS = 3
TURNS = B // STREAMS
H = 16
H0 = H // 2
PAIRS = H // 2
FT = 1024 // P
EPS = 1e-5
BIG = float(2 ** 100)
SLOT0 = 66
SLOT = 32

L0A, L0B, L1, L2, SA, CA = range(6)
PASSES = 6
SCALE = {L0A: 0.125, L0B: 0.125, L1: 0.0625, L2: 0.25, SA: 0.25, CA: 0.25}

Step = namedtuple("Step", "kind s a n u e g l")

USES = {"CT": 1, "XT": 1, "PEN": 1, "K0": 2, "Q0": 2, "V0": 2, "K": 1, "Q": 1, "V": 1, "X": 1, "MT": 1,
        "N": 1, "T0": 1, "T": 1, "O": 1, "LNa": 1, "LNb": 1, "F1": 1, "F2": 1, "OUT": 1}


def units(a):
    return H0 // 2 if a < L1 else PAIRS


def attend(s, a):
    out = []
    last = units(a) - 1
    per_group = 1 if a < L1 else 2
    done = None
    for n in range(last + 2):
        if n <= last:
            out.append(("E", s, a, n))
        if done is not None:
            out.append(("N", s, a, done))
            if a < L1 and done >= 1:
                out.append(("T0", s, a, done - 1))
            done = None
        if n >= 1:
            out.append(("PV", s, a, n - 1))
            if n % per_group == 0:
                done = n // per_group - 1
                out.append(("C", s, a, done))
    out.append(("N", s, a, done))
    if a < L1:
        out += [("T0", s, a, g) for g in (done - 1, done)]
    return out


def norm(s, v):
    return [("LNa", s, v, 0), ("LNb", s, v, 0)]


def feed(s, v):
    return [("F1", s, v, n) for n in range(FT // 2)] + [("F2", s, v, 0)]


def prepare(s, a):
    out = []
    if a == L0A:
        out += [("CT", s, a, 0), ("XT", s, a, 0), ("PEN", s, a, 0)]
    if a in (L0A, L0B):
        out += [("K0", s, a, 0), ("Q0", s, a, 0), ("V0", s, a, 0)]
        tiles = units(a)
    else:
        k_and_v = [("K", s, a, 0), ("V", s, a, 0)]
        context_out = [("T", s, a - 1, 0), ("O", s, a - 1, 0)]
        if a == L1:
            out += [("O", s, a - 1, 0)] + k_and_v + norm(s, 0)
        elif a == L2:
            out += k_and_v + context_out + norm(s, 1) + feed(s, 1) + norm(s, 2)
        elif a == SA:
            out += context_out + norm(s, 3) + norm(s, 4) + k_and_v
        else:
            out += k_and_v + context_out + norm(s, 5)
        out += [("Q", s, a, 0), ("KM", s, a, 0)]
        tiles = PAIRS
    out += [("X", s, a, n) for n in range(QT * tiles)]
    out += [("MT", s, a, 0)]
    return out


def finish(s):
    return [("T", s, CA, 0), ("O", s, CA, 0)] + norm(s, 6) + feed(s, 6) + [("OUT", s, CA, 0)]


def chain(s):
    out = prepare(s, L0A)
    for a in range(PASSES):
        out += attend(s, a)
        out += prepare(s, a + 1) if a + 1 < PASSES else finish(s)
    return out


ORDER = (
    "0000001110111001110011100101001000000000000000001111101011100001000010110101110101011001011000100111"
    "0111001000001111101110110011101011110110011110000001000011000000011111010110011001011001010001001000"
    "0000001100011111011111011111011111101111010101010110100110001011000000000001011011111110101010100011"
    "0000010000000000001101111101110111111111011110101010100110010011011000000000001110111111001011011001"
    "0100000010000000000010100111110111110111111101111001111110010011000000000011001111101111110110100000"
    "10000000000000000011011110111111101111111011101010101010111111"
)


def schedule():
    left = [chain(s) for s in range(STREAMS)]
    assert [ORDER.count(str(s)) for s in range(STREAMS)] == [len(c) for c in left]
    raw = [left[int(s)].pop(0) for s in ORDER]
    steps, u, e, g, l = [], 0, 0, 0, 0
    for kind, s, a, n in raw:
        steps.append(Step(kind, s, a, n, u, e, g, l))
        u += USES.get(kind, 0)
        e += kind == "E"
        g += kind == "N"
        l += kind == "LNa"
    return steps, u, e, g, l


STEPS, N_USES, N_UNITS, N_GROUPS, N_NORMS = schedule()
assert N_UNITS % 2 == 0 and N_GROUPS % 2 == 0
UNIT_NO = {(t.s, t.a, t.n): t.e for t in STEPS if t.kind == "E"}
GROUP_NO = {(t.s, t.a, t.n): t.g for t in STEPS if t.kind == "N"}

LAST_USE = {(t.kind, t.s, t.a, t.n): t.u + USES[t.kind] - 1 for t in STEPS if t.kind in USES}

KQ_OPS = {L0A: 0, L0B: 4, L1: 8, L2: 10, SA: 12, CA: 14}
K_DMAS = {L1: 13, L2: 12, SA: 12, CA: 12}
M_DMAS = {L1: 3, L2: 2, SA: 2, CA: 2}
Q_DMAS = 13
SUMMED_BY = {0: lambda s: ("O", s, L0B), 1: lambda s: ("O", s, L1), 2: lambda s: ("F2", s, 1),
             3: lambda s: ("O", s, L2), 5: lambda s: ("O", s, SA), 6: lambda s: ("O", s, CA)}
X_NORM = {L1: 0, L2: 2, SA: 4, CA: 5}
COLS = {}


def _columns():
    at = 0
    for name, n in (("b0q", 8), ("b0k", 8), ("b0v", 8), ("b0o", 2), ("g0", 2), ("be0", 2),
                    ("b1o", 2), ("g1", 2), ("be1", 2), ("b1f", 8), ("b1g", 2), ("g2", 2), ("be2", 2),
                    ("b2q", 2), ("b2k", 2), ("b2v", 2), ("b2o", 2), ("g3", 2), ("be3", 2),
                    ("b3q", 2), ("b3k", 2), ("b3v", 2), ("b3o", 2), ("b4q", 2), ("b4k", 2), ("b4v", 2),
                    ("b4o", 2), ("b5f", 8), ("b5g", 2),
                    ("g4", 2), ("be4", 2), ("g5", 2), ("be5", 2), ("g6", 2), ("be6", 2)):
        COLS[name] = (at, n)
        at += n
    return at


N_COLS = _columns()


def build(nc, t):
    with ExitStack() as ctx:
        def sb(name, shape, dt=F32):
            return ctx.enter_context(nc.sbuf_tensor(name, shape, dt))

        def ps(name, shape, dt=F32):
            return ctx.enter_context(nc.psum_tensor(name, shape, dt))

        class Signal:
            every = []

            def __init__(self, name, per_turn):
                self.sem = ctx.enter_context(nc.semaphore(name))
                self.per_turn = per_turn
                Signal.every.append(self)

            def at(self, turn, n):
                assert n + self.per_turn > 0, n
                return turn * self.per_turn + (self.per_turn + n)

        Signal.every = []

        def pair(name, per_turn):
            return [Signal(f"{name}_{i}", per_turn) for i in range(2)]

        w0q, w0k, w0v = (sb(n, [P, KT, 1024]) for n in ("w0q", "w0k", "w0v"))
        w0o = sb("w0o", [P, FT, D])
        w1q, w1k, w1v = (sb(n, [P, P]) for n in ("w1q", "w1k", "w1v"))
        w1o = sb("w1o", [P, KT, D])
        w1f, w1g = sb("w1f", [P, KT, 1024]), sb("w1g", [P, FT, D])
        w2q, w2k, w2v, w2o = (sb(n, [P, KT, D]) for n in ("w2q", "w2k", "w2v", "w2o"))
        w3q, w3k, w3v, w3o = (sb(n, [P, KT, D]) for n in ("w3q", "w3k", "w3v", "w3o"))
        w4q, w4k, w4v, w4o = (sb(n, [P, KT, D]) for n in ("w4q", "w4k", "w4v", "w4o"))
        w5f, w5g = sb("w5f", [P, KT, 1024]), sb("w5g", [P, FT, D])
        cols = sb("cols", [P, N_COLS])

        def col(name, i):
            return cols[:, COLS[name][0] + i:COLS[name][0] + i + 1]

        ident = sb("ident", [P, P])
        ident_b = sb("ident_b", [P, P], BF16)
        ident_r = sb("ident_r", [H, H], F32R)
        parity = sb("parity", [P, 2])
        few_rows = sb("few_rows", [P, 2, S], F32R)
        k_fixed = few_rows[0:32, :, :]
        q_fixed = few_rows[32:35, 0, :]
        pen1_row = [few_rows[64:65, s, :] for s in range(STREAMS)]
        mask1_row = [few_rows[96:97, s, :].bitcast(mybir.dt.int32) for s in range(STREAMS)]
        half = sb("half", [P, KT])
        pen3 = sb("pen3", [P, QT, S], BF16)
        pen3_t = sb("pen3_t", [P, QT, S], BF16)
        flag = sb("flag", [P, 4 * QT])

        two = range(STREAMS)
        q_st = [sb(f"q_st{s}", [P, PAIRS, S], F32R) for s in two]
        k_st = [sb(f"k_st{s}", [P, H, S], F32R) for s in two]
        inner = [sb(f"inner{s}", [P, FT, S]) for s in two]
        v_aug = [sb(f"v_aug{s}", [P, QT * H0 * SLOT0]) for s in two]
        rows = [sb(f"rows{s}", [P, QT, D]) for s in two]
        x_t = [sb(f"x_t{s}", [P, KT, S]) for s in two]
        y_t = [sb(f"y_t{s}", [P, KT, S]) for s in two]
        ctx_t = [sb(f"ctx_t{s}", [P, KT, S]) for s in two]
        mask0 = [sb(f"mask0{s}", [P, QT, S], mybir.dt.uint8) for s in two]
        pen0 = [sb(f"pen0{s}", [P, QT, S], BF16) for s in two]
        pen0_t = [sb(f"pen0_t{s}", [P, QT, S], BF16) for s in two]
        mask1_col = [sb(f"mask1_col{s}", [P, QT], mybir.dt.int32) for s in two]
        pen1_col = [sb(f"pen1_col{s}", [P, QT]) for s in two]
        neg_max = [sb(f"neg_max{s}", [P, QT, H]) for s in two]
        neg_max_t = [sb(f"neg_max_t{s}", [H, S], F32R) for s in two]
        stats = [sb(f"stats{s}", [P, QT, 6]) for s in two]
        mean_var = [sb(f"mean_var{s}", [P, QT, 2]) for s in two]
        var_eps = [sb(f"var_eps{s}", [P, QT]) for s in two]
        rstd = [sb(f"rstd{s}", [P, QT]) for s in two]

        fixed = inner[0][0:32, 0:3, :]

        def split(s, i):
            return inner[s][:, 2 * i:2 * i + 2, :].bitcast(F32R)

        Q_HI, Q_LO, K_HI, K_LO = range(4)

        def v0(s):
            return v_aug[s][:, :].rearrange("p (t h c) -> p t h c", t=QT, h=H0)

        def v16(s):
            return v_aug[s][:, 0:QT * H * SLOT].rearrange("p (t h c) -> p t h c", t=QT, h=H)

        def rows0(s, g):
            return rows[s][:, g % 2, :].rearrange("p (t c) -> p t c", t=QT)

        probs = [sb(f"probs{w}", [P, QT, 2, S]) for w in two]
        summed = [sb(f"summed{c}", [P, 2 * S]) for c in two]
        recip = [sb(f"recip{c}", [P, 2 * 4]) for c in two]

        wide = [ps(f"wide{w}", [P, QT, 2, S]) for w in two]
        acc = ps("acc", [P, 2 * S])
        misc = [ps(f"misc{b}", [P, 2, S]) for b in range(BANKS)]

        def flat(b):
            return misc[b][:, :, :].rearrange("p a b -> p (a b)")

        uses_of = [len(range(b, N_USES, BANKS)) for b in range(BANKS)]
        misc_full = [Signal(f"misc_full_{b}", n) for b, n in enumerate(uses_of)]
        misc_free = [Signal(f"misc_free_{b}", n) for b, n in enumerate(uses_of)]
        scores = pair("scores", N_UNITS // 2)
        exp_done = pair("exp_done", N_UNITS // 2)
        pv_done = pair("pv_done", N_UNITS // 2)
        summed_ready = pair("summed_ready", N_GROUPS // 2)
        recip_ready = pair("recip_ready", N_GROUPS // 2)
        bn_ready = Signal("bn_ready", N_NORMS)
        mv_ready = Signal("mv_ready", N_NORMS)
        eps_ready = Signal("eps_ready", N_NORMS)
        rstd_ready = Signal("rstd_ready", N_NORMS)
        kq_hi = pair("kq_hi", 16)
        q_dma = pair("q_dma", 16 * Q_DMAS * 4)
        k_dma = pair("k_dma", 16 * sum(K_DMAS.values()))
        fix_dma = pair("fix_dma", 16 * 2)
        k_masked = pair("k_masked", 8)
        k_zeroed = pair("k_zeroed", 2)
        m_dma = pair("m_dma", 16 * sum(M_DMAS.values()))
        ones_ready = pair("ones_ready", 2)
        pen_ready = pair("pen_ready", 3)
        load_x = pair("load_x", 16)
        load_ctx = pair("load_ctx", 16)
        load_mask = pair("load_mask", 16 * 3)
        out_dma = pair("out_dma", 16)
        primed = ctx.enter_context(nc.semaphore("primed"))
        settled = ctx.enter_context(nc.semaphore("settled"))
        w_dma = ctx.enter_context(nc.semaphore("w_dma"))
        const_ready = ctx.enter_context(nc.semaphore("const_ready"))
        flag_step = ctx.enter_context(nc.semaphore("flag_step"))
        pen3_in = ctx.enter_context(nc.semaphore("pen3_in"))
        pen3_turned = ctx.enter_context(nc.semaphore("pen3_turned"))
        bd_zeroed = ctx.enter_context(nc.semaphore("bd_zeroed"))

        N_CONST = 8
        weights = [(w0q, "w0q", KT), (w0k, "w0k", KT), (w0v, "w0v", KT), (w0o, "w0o", FT), (w1o, "w1o", KT),
                   (w1f, "w1f", KT), (w1g, "w1g", FT), (w2q, "w2q", KT), (w2k, "w2k", KT), (w2v, "w2v", KT),
                   (w2o, "w2o", KT), (w3q, "w3q", KT), (w3k, "w3k", KT), (w3v, "w3v", KT), (w3o, "w3o", KT),
                   (w4q, "w4q", KT), (w4k, "w4k", KT), (w4v, "w4v", KT), (w4o, "w4o", KT),
                   (w5f, "w5f", KT), (w5g, "w5g", FT)]
        N_W = 16 * (len(weights) + 5 + 3 * 8)
        mask3 = mask0[0]

        def last_unit(s, a):
            if a == L0A:
                return UNIT_NO[s, CA, units(CA) - 1] - N_UNITS
            return UNIT_NO[s, a - 1, units(a - 1) - 1]

        def wait_scores_read(eng, i, s, a):
            e = last_unit(s, a)
            eng.wait_ge(exp_done[e % 2].sem, exp_done[e % 2].at(i, e // 2 + 1))

        def wait_v_read(eng, i, s, a):
            e = last_unit(s, a)
            eng.wait_ge(pv_done[e % 2].sem, pv_done[e % 2].at(i, e // 2 + 1))

        def wait_misc_full(eng, i, u):
            eng.wait_ge(misc_full[u % BANKS].sem, misc_full[u % BANKS].at(i, u // BANKS + 1))

        def wait_misc_free(eng, i, u):
            eng.wait_ge(misc_free[u % BANKS].sem, misc_free[u % BANKS].at(i, u // BANKS))

        def wait_result(eng, i, kind, s, a, n=0):
            u = LAST_USE[kind, s, a, n]
            eng.wait_ge(misc_free[u % BANKS].sem, misc_free[u % BANKS].at(i, u // BANKS + 1))

        def wait_k_stacked(eng, i, s, a):
            eng.wait_ge(k_dma[s].sem, k_dma[s].at(i, 16 * sum(K_DMAS[x] for x in range(L1, a + 1))))

        def settle(eng):
            eng.sem_inc(settled, 1)

        block = ctx.enter_context(nc.Block())

        @block.sync
        def _(sp):
            for tile, name, n in weights:
                sp.dma_start(tile[:, :, :], t[name].rearrange("(k p) n -> p k n", p=P)).then_inc(w_dma, 16)
            sp.dma_start(cols[:, :], t["cols"]).then_inc(w_dma, 16)
            sp.dma_start(ident[:, :], t["ident"]).then_inc(w_dma, 16)
            sp.dma_start(parity[:, :], t["parity"]).then_inc(w_dma, 16)
            sp.dma_start(fixed, t["fixed"]).then_inc(w_dma, 16)
            sp.dma_start(mask3[:, :, :], t["mask3"].rearrange("(t p) k -> p t k", p=P)).then_inc(w_dma, 16)
            sp.wait_ge(bd_zeroed, 3)
            for tile, name in ((w1q, "w1q"), (w1k, "w1k"), (w1v, "w1v")):
                for h in range(8):
                    sp.dma_start(tile[16 * h:16 * h + 16, 16 * h:16 * h + 16], t[name]).then_inc(w_dma, 16)
            sp.wait_ge(primed, 1)
            sp.wait_ge(flag_step, 3)
            sp.wait_ge(const_ready, N_CONST)

            with sp.Fori(0, TURNS) as i:
                for s in two:
                    b = i * STREAMS + s
                    sp.wait_ge(out_dma[s].sem, out_dma[s].at(i, 0))
                    settle(sp)
                    sp.dma_start(rows[s][:, :, :], t["ctx"][bass.ds(b, 1)].rearrange("b (t p) d -> p (b t) d", p=P)
                                 ).then_inc(load_ctx[s].sem, 16)
                    sp.dma_start(y_t[s][:, :, :], t["x"][bass.ds(b, 1)].rearrange("b (t p) d -> p (b t) d", p=P)
                                 ).then_inc(load_x[s].sem, 16)
                    sp.dma_start(mask0[s][:, :, :], t["mask0"][bass.ds(b, 1)].rearrange("b (t p) k -> p (b t) k", p=P)
                                 ).then_inc(load_mask[s].sem, 16)
                    sp.dma_start(mask1_row[s], t["mask1"][bass.ds(b, 1)]).then_inc(load_mask[s].sem, 16)
                    sp.dma_start(mask1_col[s][:, :], t["mask1_cols"][bass.ds(b, 1)].rearrange("b p t -> p (b t)")
                                 ).then_inc(load_mask[s].sem, 16)
                for st in STEPS:
                    s, a = st.s, st.a
                    if st.kind == "K":
                        wait_scores_read(sp, i, s, a)
                        settle(sp)
                        if a == L1:
                            for j in range(2):
                                sp.dma_start(k_st[s][96:128, j::2, :].bitcast(F32),
                                             k_fixed[:, j:j + 1, :].bitcast(F32).to_broadcast([32, PAIRS, S])
                                             ).then_inc(fix_dma[s].sem, 16)
                        wait_result(sp, i, "K", s, a)
                        for p4 in range(4):
                            r = slice(32 * p4, 32 * p4 + 32)
                            for term, part in enumerate((K_HI, K_HI, K_LO)):
                                sp.dma_start(k_st[s][32 * term:32 * term + 32, 2 * p4::8, :].bitcast(F32),
                                             split(s, part)[r].bitcast(F32)
                                             ).then_inc(k_dma[s].sem, 16)
                        if a == L1:
                            sp.wait_ge(fix_dma[s].sem, fix_dma[s].at(i, 32))
                            settle(sp)
                            sp.wait_ge(pen_ready[s].sem, pen_ready[s].at(i, 3))
                            sp.dma_start(k_st[s][98:99, :, :].bitcast(F32),
                                         pen1_row[s].bitcast(F32).unsqueeze(1).to_broadcast([1, H, S])
                                         ).then_inc(k_dma[s].sem, 16)
                    elif st.kind == "Q":
                        n = 3 if a == L1 else 2
                        sp.dma_start(q_st[s][96:96 + n, :, :].bitcast(F32),
                                     q_fixed[0:n, :].bitcast(F32).unsqueeze(1).to_broadcast([n, PAIRS, S])
                                     ).then_inc(q_dma[s].sem, 16)
                        sp.wait_ge(kq_hi[s].sem, kq_hi[s].at(i, KQ_OPS[a] + 2))
                        for term, part in ((0, Q_HI), (2, Q_HI), (1, Q_LO)):
                            if part == Q_LO:
                                wait_result(sp, i, "Q", s, a)
                            for p4 in range(4):
                                r = slice(32 * p4, 32 * p4 + 32)
                                sp.dma_start(q_st[s][32 * term:32 * term + 32, p4::4, :].bitcast(F32),
                                             split(s, part)[r].bitcast(F32)
                                             ).then_inc(q_dma[s].sem, 16)
                    elif st.kind == "MT" and a >= L1:
                        wait_result(sp, i, "MT", s, a)
                        for j in range(2):
                            sp.dma_start(q_st[s][96 + j:97 + j, :, :].bitcast(F32),
                                         neg_max_t[s][8 * j:8 * j + 8, :].bitcast(F32)
                                         ).then_inc(m_dma[s].sem, 16)
                        if a == L1:
                            sp.dma_start(k_st[s][98:99, :, :].bitcast(F32),
                                         q_fixed[0:1, :].bitcast(F32).unsqueeze(1).to_broadcast([1, H, S])
                                         ).then_inc(m_dma[s].sem, 16)
                    elif st.kind == "OUT":
                        b = i * STREAMS + s
                        wait_result(sp, i, "OUT", s, a)
                        settle(sp)
                        sp.dma_start(t["out"][bass.ds(b, 1)].rearrange("b (t p) d -> p (b t) d", p=P), rows[s][:, :, :]
                                     ).then_inc(out_dma[s].sem, 16)
            for s in two:
                sp.wait_ge(out_dma[s].sem, out_dma[s].per_turn * (TURNS + 1))

        @block.gpsimd
        def _(pool):
            for sig in Signal.every:
                pool.sem_inc(sig.sem, sig.per_turn)
            pool.sem_inc(primed, 1)
            for tile in (w1q, w1k, w1v):
                nc.gpsimd.memset(tile[:, :], 0.0).then_inc(bd_zeroed, 1)
            nc.gpsimd.memset(half[:, :], -0.5).then_inc(const_ready, 1)
            for s in two:
                nc.gpsimd.memset(neg_max[s][:, :, :], 0.0).then_inc(const_ready, 1)
                nc.gpsimd.memset(v_aug[s][:, :], 0.0).then_inc(const_ready, 1)
            pool.wait_ge(const_ready, N_CONST)

            with pool.Fori(0, TURNS) as i:
                before = rstd_ready, 0
                for st in STEPS:
                    s, a = st.s, st.a
                    if st.kind == "K0" and a == L0A:
                        wait_scores_read(pool, i, s, a)
                        settle(pool)
                        pool.wait_ge(before[0].sem, before[0].at(i, before[1]))
                        settle(pool)
                        nc.gpsimd.memset(k_st[s][64:128, 0::2, :].bitcast(F32), 0.0).then_inc(k_zeroed[s].sem, 1)
                        pool.wait_ge(k_zeroed[s].sem, k_zeroed[s].at(i, 1))
                        settle(pool)
                        nc.gpsimd.memset(k_st[s][0:64, 1::2, :].bitcast(F32), 0.0).then_inc(k_zeroed[s].sem, 1)
                        pool.wait_ge(k_zeroed[s].sem, k_zeroed[s].at(i, 2))
                        settle(pool)
                    elif st.kind == "V0" and a == L0A:
                        wait_v_read(pool, i, s, a)
                        settle(pool)
                        nc.gpsimd.memset(v0(s)[:, :, :, 64:66], 1.0).then_inc(ones_ready[s].sem, 1)
                        before = ones_ready[s], 1
                    elif st.kind == "V" and a == L1:
                        wait_v_read(pool, i, s, a)
                        settle(pool)
                        nc.gpsimd.memset(v16(s)[:, :, :, 16:17], 1.0).then_inc(ones_ready[s].sem, 1)
                        before = ones_ready[s], 2
                    elif st.kind == "LNa":
                        pool.wait_ge(mv_ready.sem, mv_ready.at(i, st.l + 1))
                        settle(pool)
                        nc.gpsimd.tensor_scalar(var_eps[s][:, :], mean_var[s][:, :, 1], EPS, None, ALU.add
                                                ).then_inc(eps_ready.sem, 1)
                        pool.wait_ge(eps_ready.sem, eps_ready.at(i, st.l + 1))
                        nc.gpsimd.tensor_tensor(rstd[s][:, :], var_eps[s][:, :], half[:, :], ALU.pow
                                                ).then_inc(rstd_ready.sem, 1)
                        before = rstd_ready, st.l + 1

        @block.tensor
        def _(pe):
            mm = nc.tensor.matmul
            turn = nc.tensor.transpose
            pe.wait_ge(primed, 1)
            pe.wait_ge(w_dma, N_W)
            pe.wait_ge(const_ready, N_CONST)
            pe.wait_ge(pen3_in, 1)
            for kt in range(QT):
                for qt in range(QT):
                    ins = turn(flat(0).bitcast(BF16)[:, kt * S + qt * P:kt * S + qt * P + P],
                               pen3[:, qt, kt * P:kt * P + P], ident_b[:, :])
            ins.then_inc(pen3_turned, 1)
            pe.wait_ge(pen3_turned, 2)

            def wait_made(i, u, kind, s, a, n=0):
                if LAST_USE[kind, s, a, n] % BANKS != u % BANKS:
                    wait_result(pe, i, kind, s, a, n)

            def project(b, w, x, tiles):
                for half_, m in enumerate(tiles):
                    n = w.shape[1]
                    for k in range(n):
                        ins = mm(misc[b][:, half_, :], w[:, k, m * P:m * P + P], x[:, k, :],
                                 start=k == 0, stop=k == n - 1)
                return ins

            def turn_square(b, src):
                for i_ in range(2):
                    for j_ in range(2):
                        ins = turn(misc[b][:, j_, i_ * P:i_ * P + P], src[:, i_, j_ * P:j_ * P + P], ident[:, :])
                return ins

            def product_with_v(i, s, a, n):
                e = UNIT_NO[s, a, n]
                w = e % 2
                g = GROUP_NO[s, a, n if a < L1 else n // 2]
                pe.wait_ge(exp_done[w].sem, exp_done[w].at(i, e // 2 + 1))
                if n == 0:
                    wait_result(pe, i, "V0" if a < L1 else "V", s, a)
                    pe.wait_ge(ones_ready[s].sem, ones_ready[s].at(i, 1 if a < L1 else 2))
                if a < L1 or n % 2 == 0:
                    pe.wait_ge(summed_ready[(g - 1) % 2].sem, summed_ready[(g - 1) % 2].at(i, (g - 1) // 2 + 1))
                for kt in range(QT):
                    for j in range(2):
                        if a < L1:
                            out, v = acc[0:SLOT0, j * S:j * S + S], v0(s)[:, kt, 2 * n + j, :]
                        else:
                            r = SLOT * ((2 * n + j) % 4)
                            out, v = acc[r:r + SLOT, 0:S], v16(s)[:, kt, 2 * n + j, :]
                        ins = mm(out, v, probs[w][:, kt, j, :], start=kt == 0 and (a >= L1 or j == 0),
                                 stop=kt == QT - 1, skip_group_check=True)
                ins.then_inc(pv_done[w].sem, 1)

            with pe.Fori(0, TURNS) as i:
                for st in STEPS:
                    s, a, n, u = st.s, st.a, st.n, st.u
                    b = u % BANKS
                    kind = st.kind
                    if kind == "PV":
                        product_with_v(i, s, a, n)
                        continue
                    if kind == "E":
                        w = st.e % 2
                        if n == 0:
                            wait_result(pe, i, "MT", s, a)
                            if a >= L1:
                                total = 16 * sum(M_DMAS[x] for x in range(L1, a + 1))
                                pe.wait_ge(m_dma[s].sem, m_dma[s].at(i, total))
                        pe.wait_ge(exp_done[w].sem, exp_done[w].at(i, st.e // 2))
                        pen = {L0A: pen0_t[s], L0B: pen0_t[s], SA: pen3_t}.get(a)
                        for kt in range(QT):
                            keys = slice(kt * P, kt * P + P)
                            if pen is not None:
                                ins = mm(wide[w][:, kt, :, :], ident_b[:, :],
                                         pen[:, kt:kt + 1, :].to_broadcast([P, 2, S]),
                                         start=True, stop=False, skip_group_check=True)
                            for j in range(2):
                                out = wide[w][:, kt, j, :]
                                first = pen is None and j == 0
                                if a < L1:
                                    for kk, qq in ((2 * n + j, n), (2 * n + j, 4 + n), (8 + 2 * n + j, n)):
                                        mm(out, k_st[s][:, kk, keys], q_st[s][:, qq, :],
                                           start=False, stop=False, skip_group_check=True)
                                    r = 8 * j + n
                                    ins = mm(out, ident_r[:, r:r + 1].to_broadcast([H, P]), neg_max_t[s][:, :],
                                             start=False, stop=True, skip_group_check=True)
                                else:
                                    ins = mm(out, k_st[s][:, 2 * n + j, keys], q_st[s][:, n, :],
                                             start=first, stop=True, skip_group_check=True)
                        ins.then_inc(scores[w].sem, 1)
                        continue
                    if kind in ("KM", "C"):
                        continue
                    wait_misc_free(pe, i, u)
                    if kind == "CT":
                        pe.wait_ge(load_ctx[s].sem, load_ctx[s].at(i, 16))
                        ins = turn_square(b, rows[s])
                    elif kind == "XT":
                        pe.wait_ge(load_x[s].sem, load_x[s].at(i, 16))
                        ins = turn_square(b, y_t[s])
                    elif kind == "PEN":
                        pe.wait_ge(pen_ready[s].sem, pen_ready[s].at(i, 1))
                        for kt in range(QT):
                            for qt in range(QT):
                                ins = turn(flat(b).bitcast(BF16)[:, kt * S + qt * P:kt * S + qt * P + P],
                                           pen0[s][:, qt, kt * P:kt * P + P], ident_b[:, :])
                    elif kind in ("K0", "Q0"):
                        if kind == "K0":
                            wait_made(i, u, "CT", s, L0A)
                        else:
                            wait_made(i, u, "XT", s, L0A)
                        for r in range(2):
                            if r:
                                ins.then_inc(misc_full[b].sem, 1)
                                b = (u + 1) % BANKS
                                wait_misc_free(pe, i, u + 1)
                            t0 = 4 * a + 2 * r
                            ins = project(b, w0k if kind == "K0" else w0q, ctx_t[s] if kind == "K0" else x_t[s],
                                          (t0, t0 + 1))
                    elif kind == "V0":
                        for tt in range(QT):
                            if tt:
                                ins.then_inc(misc_full[b].sem, 1)
                                b = (u + 1) % BANKS
                                wait_misc_free(pe, i, u + 1)
                            for k in range(KT):
                                ins = mm(flat(b), ctx_t[s][:, k, tt * P:tt * P + P], w0v[:, k, 512 * a:512 * a + 512],
                                         start=k == 0, stop=k == KT - 1)
                    elif kind in ("K", "Q"):
                        if kind == "Q" or a == SA:
                            wait_made(i, u, "LNb", s, X_NORM[a])
                        x = x_t[s] if kind == "Q" or a == SA else ctx_t[s]
                        if a == L1:
                            for m in range(KT):
                                ins = mm(misc[b][:, m, :], (w1q if kind == "Q" else w1k)[:, :], x[:, m, :],
                                         start=True, stop=True)
                        else:
                            w = {"Q": {L2: w2q, SA: w3q, CA: w4q}, "K": {L2: w2k, SA: w3k, CA: w4k}}[kind][a]
                            ins = project(b, w, x, (0, 1))
                    elif kind == "V":
                        x = x_t[s] if a == SA else ctx_t[s]
                        for tt in range(QT):
                            tok = slice(tt * P, tt * P + P)
                            if a == L1:
                                for k in range(KT):
                                    ins = mm(misc[b][:, tt, k * P:k * P + P], x[:, k, tok], w1v[:, :],
                                             start=True, stop=True)
                            else:
                                w = {L2: w2v, SA: w3v, CA: w4v}[a]
                                for k in range(KT):
                                    ins = mm(misc[b][:, tt, :], x[:, k, tok], w[:, k, :], start=k == 0, stop=k == KT - 1)
                    elif kind == "X":
                        pairs = units(a)
                        qt, p = n // pairs, n % pairs
                        if n == 0:
                            if a < L1:
                                wait_made(i, u, "Q0", s, a)
                                pe.wait_ge(k_zeroed[s].sem, k_zeroed[s].at(i, 2))
                            else:
                                pe.wait_ge(q_dma[s].sem, q_dma[s].at(i, 16 * Q_DMAS * (a - L1 + 1)))
                                pe.wait_ge(k_masked[s].sem, k_masked[s].at(i, 2 * (a - L1 + 1)))
                        rows_q = slice(qt * P, qt * P + P)
                        pen = {L0A: pen0[s], L0B: pen0[s], SA: pen3}.get(a)
                        if pen is not None:
                            mm(misc[b][:, :, :], ident_b[:, :], pen[:, qt:qt + 1, :].to_broadcast([P, 2, S]),
                               start=True, stop=False)
                        if a < L1:
                            for qq, kk in ((p, 2 * p), (4 + p, 2 * p), (p, 8 + 2 * p)):
                                ins = mm(misc[b][:, :, :], q_st[s][:, qq, rows_q], k_st[s][:, kk:kk + 2, :],
                                         start=pen is None and kk < 8 and qq < 4, stop=kk >= 8)
                        else:
                            ins = mm(misc[b][:, :, :], q_st[s][:, p, rows_q], k_st[s][:, 2 * p:2 * p + 2, :],
                                     start=pen is None, stop=True)
                    elif kind == "MT":
                        wait_made(i, u, "X", s, a, QT * units(a) - 1)
                        for qt in range(QT):
                            ins = turn(misc[b][0:H, 0, qt * P:qt * P + P], neg_max[s][:, qt, :], ident[:, :])
                    elif kind == "N":
                        g = st.g
                        pe.wait_ge(summed_ready[g % 2].sem, summed_ready[g % 2].at(i, g // 2 + 1))
                        for qt in range(QT):
                            if a < L1:
                                for j in range(2):
                                    at = SLOT0 * (2 * qt + j)
                                    ins = turn(flat(b)[:, at:at + SLOT0],
                                               summed[g % 2][0:SLOT0, j * S + qt * P:j * S + qt * P + P],
                                               ident[0:SLOT0, 0:SLOT0])
                            else:
                                ins = turn(misc[b][:, 0, qt * P:qt * P + P], summed[g % 2][:, qt * P:qt * P + P],
                                           ident[:, :])
                    elif kind == "T0":
                        wait_made(i, u, "N", s, a, n)
                        for qt in range(QT):
                            ins = turn(misc[b][:, 0, qt * P:qt * P + P], rows0(s, n)[:, qt, :], ident[:, :])
                    elif kind == "T":
                        wait_made(i, u, "N", s, a, 3)
                        ins = turn_square(b, rows[s])
                    elif kind == "O":
                        wait_made(i, u, *(("T0", s, a, 3) if a < L1 else ("T", s, a)))
                        w = {L0B: w0o, L1: w1o, L2: w2o, SA: w3o, CA: w4o}[a]
                        ins = project(b, w, inner[s], (0, 1))
                    elif kind == "LNa":
                        if a == 4:
                            wait_made(i, u, "LNb", s, 3)
                        else:
                            wait_made(i, u, *SUMMED_BY[a](s))
                        ins = turn_square(b, y_t[s])
                    elif kind == "LNb":
                        wait_made(i, u, "LNa", s, a)
                        ins = turn_square(b, rows[s])
                    elif kind == "F1":
                        if n == 0:
                            wait_made(i, u, "LNb", s, a)
                        ins = project(b, w1f if a == 1 else w5f, x_t[s], (2 * n, 2 * n + 1))
                    elif kind == "F2":
                        wait_made(i, u, "F1", s, a, 3)
                        if LAST_USE["F1", s, a, 2] % BANKS != LAST_USE["F1", s, a, 3] % BANKS:
                            wait_made(i, u, "F1", s, a, 2)
                        ins = project(b, w1g if a == 1 else w5g, inner[s], (0, 1))
                    elif kind == "OUT":
                        wait_made(i, u, "F2", s, 6)
                        ins = turn_square(b, y_t[s])
                    ins.then_inc(misc_full[b].sem, 1)

        @block.scalar
        def _(act):
            fn = nc.scalar.activation
            act.wait_ge(primed, 1)
            act.wait_ge(w_dma, N_W)
            act.wait_ge(const_ready, N_CONST)
            act.wait_ge(flag_step, 3)

            with act.Fori(0, TURNS) as i:
                for st in STEPS:
                    s, a, n, u = st.s, st.a, st.n, st.u
                    b = u % BANKS
                    kind = st.kind
                    if kind == "E":
                        w = st.e % 2
                        act.wait_ge(scores[w].sem, scores[w].at(i, st.e // 2 + 1))
                        act.wait_ge(pv_done[w].sem, pv_done[w].at(i, st.e // 2))
                        if a == L1:
                            for kt in range(QT):
                                ins = fn(probs[w][:, kt, :, :], wide[w][:, kt, :, :], ACT.Exp,
                                         bias=pen1_col[s][:, kt:kt + 1], scale=SCALE[a])
                        else:
                            ins = fn(probs[w][:, :, :, :], wide[w][:, :, :, :], ACT.Exp, scale=SCALE[a])
                        ins.then_inc(exp_done[w].sem, 1)
                    elif kind == "C":
                        g = GROUP_NO[s, a, n]
                        e = UNIT_NO[s, a, n if a < L1 else 2 * n + 1]
                        act.wait_ge(pv_done[e % 2].sem, pv_done[e % 2].at(i, e // 2 + 1))
                        if a < L1:
                            ins = nc.scalar.copy(summed[g % 2][0:SLOT0, :], acc[0:SLOT0, :])
                        else:
                            ins = nc.scalar.copy(summed[g % 2][:, 0:S], acc[:, 0:S])
                        ins.then_inc(summed_ready[g % 2].sem, 1)
                    elif kind in ("CT", "XT"):
                        wait_misc_full(act, i, u)
                        dst = ctx_t[s] if kind == "CT" else x_t[s]
                        nc.scalar.copy(dst[:, :, :], misc[b][:, :, :]).then_inc(misc_free[b].sem, 1)
                    elif kind == "K0":
                        wait_scores_read(act, i, s, a)
                        for r in range(2):
                            b = (u + r) % BANKS
                            wait_misc_full(act, i, u + r)
                            for half_ in range(2):
                                tile = 2 * r + half_
                                for j in range(2):
                                    rr = slice(64 * j, 64 * j + 64)
                                    c = COLS["b0k"][0] + 4 * a + tile
                                    ins = fn(k_st[s][rr, 2 * tile + j, :], misc[b][rr, half_, :], ACT.Identity,
                                             bias=cols[rr, c:c + 1])
                            ins.then_inc(kq_hi[s].sem, 1)
                    elif kind == "Q0":
                        for r in range(2):
                            b = (u + r) % BANKS
                            wait_misc_full(act, i, u + r)
                            for half_ in range(2):
                                tile = 2 * r + half_
                                ins = fn(q_st[s][:, tile, :], misc[b][:, half_, :], ACT.Identity,
                                         bias=col("b0q", 4 * a + tile))
                            ins.then_inc(kq_hi[s].sem, 1)
                    elif kind in ("K", "Q"):
                        wait_misc_full(act, i, u)
                        part = split(s, K_HI if kind == "K" else Q_HI)
                        for m in range(KT):
                            if a == L1:
                                ins = nc.scalar.activation(part[:, m, :], misc[b][:, m, :], ACT.Identity)
                            else:
                                name = {L2: "b2", SA: "b3", CA: "b4"}[a] + kind.lower()
                                ins = fn(part[:, m, :], misc[b][:, m, :], ACT.Identity, bias=col(name, m))
                        ins.then_inc(kq_hi[s].sem, 1)
                    elif kind == "KM":
                        wait_k_stacked(act, i, s, a)
                        both = k_st[s][0:96, 0:H // 2:2, :]
                        fn(k_st[s][0:96, 1:H // 2:2, :], both.bitcast(F32), ACT.Identity, scale=parity[0:96, 1:2])
                        fn(both, both.bitcast(F32), ACT.Identity, scale=parity[0:96, 0:1]
                           ).then_inc(k_masked[s].sem, 1)
                    elif kind == "V0":
                        wait_v_read(act, i, s, a)
                        for tt in range(QT):
                            b = (u + tt) % BANKS
                            wait_misc_full(act, i, u + tt)
                            nc.scalar.copy(v0(s)[:, tt, :, 0:64], flat(b).rearrange("p (h c) -> p h c", h=H0)
                                           ).then_inc(misc_free[b].sem, 1)
                    elif kind == "V":
                        wait_v_read(act, i, s, a)
                        wait_misc_full(act, i, u)
                        nc.scalar.copy(v16(s)[:, :, :, 0:16], misc[b][:, :, :].rearrange("p t (h c) -> p t h c", h=H)
                                       ).then_inc(misc_free[b].sem, 1)
                    elif kind == "MT":
                        wait_misc_full(act, i, u)
                        nc.scalar.copy(neg_max_t[s][:, :], misc[b][0:H, 0, :]).then_inc(misc_free[b].sem, 1)
                    elif kind == "T0":
                        wait_misc_full(act, i, u)
                        fn(inner[s][:, 4 * a + n, :], misc[b][:, 0, :], ACT.Identity, bias=col("b0v", 4 * a + n)
                           ).then_inc(misc_free[b].sem, 1)
                    elif kind == "T":
                        wait_misc_full(act, i, u)
                        for m in range(KT):
                            if a == L1:
                                ins = nc.scalar.activation(inner[s][:, m, :], misc[b][:, m, :], ACT.Identity)
                            else:
                                ins = fn(inner[s][:, m, :], misc[b][:, m, :], ACT.Identity,
                                         bias=col({L2: "b2v", SA: "b3v", CA: "b4v"}[a], m))
                        ins.then_inc(misc_free[b].sem, 1)
                    elif kind == "LNb":
                        wait_misc_full(act, i, u)
                        dst = y_t[s] if a == 3 else x_t[s]
                        for m in range(KT):
                            ins = fn(dst[:, m, :], misc[b][:, m, :], ACT.Identity, bias=col(f"be{a}", m),
                                     scale=col(f"g{a}", m))
                        ins.then_inc(misc_free[b].sem, 1)
                    elif kind == "F1" and n % 2 == 0:
                        wait_misc_full(act, i, u)
                        if a == 1 and n == 2:
                            wait_k_stacked(act, i, s, L2)
                        for half_ in range(2):
                            m = 2 * n + half_
                            ins = fn(inner[s][:, m, :], misc[b][:, half_, :], ACT.Relu,
                                     bias=col("b1f" if a == 1 else "b5f", m))
                        ins.then_inc(misc_free[b].sem, 1)
                    elif kind == "OUT":
                        wait_misc_full(act, i, u)
                        for tt in range(QT):
                            ins = fn(rows[s][:, tt, :], misc[b][:, tt, :], ACT.Identity, bias=flag[:, 4 + tt:5 + tt])
                        ins.then_inc(misc_free[b].sem, 1)

        @block.vector
        def _(dve):
            v = nc.vector
            dve.wait_ge(primed, 1)
            dve.wait_ge(w_dma, N_W)
            v.tensor_copy(ident_b[:, :], ident[:, :]).then_inc(const_ready, 1)
            v.tensor_copy(ident_r[:, :], ident[0:H, 0:H])
            v.tensor_copy(k_fixed, fixed[:, 0:2, :]).then_inc(const_ready, 1)
            v.tensor_copy(q_fixed, fixed[0:3, 2, :]).then_inc(const_ready, 1)
            v.tensor_scalar(pen3[:, :, :], mask3[:, :, :], BIG, -BIG, ALU.mult, ALU.add).then_inc(pen3_in, 1)
            v.tensor_reduce(flag[:, 0:2], mask3[:, :, :], AX_X, ALU.max).then_inc(flag_step, 1)
            dve.wait_ge(flag_step, 1)
            v.reciprocal(flag[:, 2:4], flag[:, 0:2]).then_inc(flag_step, 1)
            dve.wait_ge(flag_step, 2)
            v.tensor_scalar(flag[:, 4:6], flag[:, 2:4], 0.0, None, ALU.mult).then_inc(flag_step, 1)
            dve.wait_ge(pen3_turned, 1)
            v.tensor_copy(pen3_t[:, :, :].rearrange("p t q -> p (t q)"), flat(0).bitcast(BF16)[:, 0:QT * S]
                          ).then_inc(pen3_turned, 1)
            dve.wait_ge(const_ready, N_CONST)

            with dve.Fori(0, TURNS) as i:
                for st in STEPS:
                    s, a, n, u = st.s, st.a, st.n, st.u
                    b = u % BANKS
                    kind = st.kind
                    if kind == "PEN":
                        dve.wait_ge(load_mask[s].sem, load_mask[s].at(i, 16 * 3))
                        v.tensor_scalar(pen0[s][:, :, :], mask0[s][:, :, :], -BIG, None, ALU.mult
                                        ).then_inc(pen_ready[s].sem, 1)
                        v.tensor_scalar(pen1_row[s], mask1_row[s], 0.0, -BIG, ALU.is_equal, ALU.mult
                                        ).then_inc(pen_ready[s].sem, 1)
                        v.tensor_scalar(pen1_col[s][:, :], mask1_col[s][:, :], 0.0, -BIG * SCALE[L1], ALU.is_equal, ALU.mult
                                        ).then_inc(pen_ready[s].sem, 1)
                        wait_misc_full(dve, i, u)
                        v.tensor_copy(pen0_t[s][:, :, :].rearrange("p t q -> p (t q)"), flat(b).bitcast(BF16)[:, 0:QT * S]
                                      ).then_inc(misc_free[b].sem, 1)
                    elif kind in ("K0", "Q0"):
                        for r in range(2):
                            b = (u + r) % BANKS
                            no = KQ_OPS[a] + (0 if kind == "K0" else 2) + r + 1
                            dve.wait_ge(kq_hi[s].sem, kq_hi[s].at(i, no))
                            for half_ in range(2):
                                tile = 2 * r + half_
                                if kind == "K0":
                                    for j in range(2):
                                        rr = slice(64 * j, 64 * j + 64)
                                        c = COLS["b0k"][0] + 4 * a + tile
                                        ins = v.scalar_tensor_tensor(
                                            k_st[s][rr, 8 + 2 * tile + j, :], misc[b][rr, half_, :], cols[rr, c:c + 1],
                                            k_st[s][rr, 2 * tile + j, :].bitcast(F32), ALU.add, ALU.subtract)
                                else:
                                    ins = v.scalar_tensor_tensor(
                                        q_st[s][:, 4 + tile, :], misc[b][:, half_, :], col("b0q", 4 * a + tile),
                                        q_st[s][:, tile, :].bitcast(F32), ALU.add, ALU.subtract)
                            ins.then_inc(misc_free[b].sem, 1)
                    elif kind in ("K", "Q"):
                        no = KQ_OPS[a] + (1 if kind == "K" else 2)
                        dve.wait_ge(kq_hi[s].sem, kq_hi[s].at(i, no))
                        hi, lo = (K_HI, K_LO) if kind == "K" else (Q_HI, Q_LO)
                        for m in range(KT):
                            hi_m = split(s, hi)[:, m, :].bitcast(F32)
                            if a == L1:
                                ins = v.tensor_tensor(split(s, lo)[:, m, :], misc[b][:, m, :], hi_m, ALU.subtract)
                            else:
                                name = {L2: "b2", SA: "b3", CA: "b4"}[a] + kind.lower()
                                ins = v.scalar_tensor_tensor(split(s, lo)[:, m, :], misc[b][:, m, :], col(name, m),
                                                             hi_m, ALU.add, ALU.subtract)
                        ins.then_inc(misc_free[b].sem, 1)
                    elif kind == "KM":
                        wait_k_stacked(dve, i, s, a)
                        both = k_st[s][0:96, H // 2::2, :]
                        v.tensor_scalar(k_st[s][0:96, H // 2 + 1::2, :], both.bitcast(F32), parity[0:96, 1:2], None,
                                        ALU.mult)
                        v.tensor_scalar(both, both.bitcast(F32), parity[0:96, 0:1], None, ALU.mult
                                        ).then_inc(k_masked[s].sem, 1)
                    elif kind == "X":
                        pairs = units(a)
                        qt, p = n // pairs, n % pairs
                        wait_misc_full(dve, i, u)
                        ins = v.tensor_reduce(neg_max[s][:, qt, p:p + 9:8], misc[b][:, :, :], AX_X, ALU.max, negate=True)
                        ins.then_inc(misc_free[b].sem, 1)
                    elif kind == "N":
                        g = st.g
                        wait_misc_full(dve, i, u)
                        if a < L1:
                            src = flat(b)[:, 0:4 * SLOT0].rearrange("p (m c) -> p m c", m=4)
                            m, width = 4, 64
                            dst = rows0(s, n).rearrange("p t (j c) -> p (t j) c", j=2)
                        else:
                            src = flat(b)[:, 0:S].rearrange("p (m c) -> p m c", c=SLOT)
                            m, width = 8, 16
                            dst = rows[s][:, :, 64 * n:64 * n + 64].rearrange("p t (j c) -> p t j c", j=4)
                        v.reciprocal(recip[g % 2][:, 0:m], src[:, :, width]).then_inc(recip_ready[g % 2].sem, 1)
                        dve.wait_ge(recip_ready[g % 2].sem, recip_ready[g % 2].at(i, g // 2 + 1))
                        if a < L1:
                            ins = v.tensor_tensor(dst, src[:, :, 0:width],
                                                  recip[g % 2][:, 0:m].unsqueeze(2).to_broadcast([P, m, width]), ALU.mult)
                        else:
                            src4 = flat(b)[:, 0:S].rearrange("p (t j c) -> p t j c", t=2, c=SLOT)
                            r4 = recip[g % 2][:, 0:8].rearrange("p (t j) -> p t j", t=2).unsqueeze(3)
                            ins = v.tensor_tensor(dst, src4[:, :, :, 0:16], r4.to_broadcast([P, 2, 4, 16]), ALU.mult)
                        ins.then_inc(misc_free[b].sem, 1)
                    elif kind in ("O", "F2"):
                        wait_misc_full(dve, i, u)
                        if kind == "F2":
                            bias, res, no = ("b1g", x_t, 3) if a == 1 else ("b5g", y_t, 7)
                        else:
                            bias = {L0B: "b0o", L1: "b1o", L2: "b2o", SA: "b3o", CA: "b4o"}[a]
                            res = y_t if a >= SA else x_t
                            no = {L0B: 1, L1: 2, L2: 4, SA: 5, CA: 6}[a]
                        for m in range(KT):
                            ins = v.scalar_tensor_tensor(y_t[s][:, m, :], misc[b][:, m, :], col(bias, m), res[s][:, m, :],
                                                         ALU.add, ALU.add)
                        ins.then_inc(misc_free[b].sem, 1)
                    elif kind == "LNa":
                        wait_misc_full(dve, i, u)
                        for tt in range(QT):
                            ins = v.bn_stats(stats[s][:, tt, :], misc[b][:, tt, :])
                        ins.then_inc(bn_ready.sem, 1)
                        dve.wait_ge(bn_ready.sem, bn_ready.at(i, st.l + 1))
                        settle(dve)
                        for tt in range(QT):
                            ins = v.bn_aggr(mean_var[s][:, tt, :], stats[s][:, tt, :])
                        ins.then_inc(mv_ready.sem, 1)
                        dve.wait_ge(rstd_ready.sem, rstd_ready.at(i, st.l + 1))
                        for tt in range(QT):
                            ins = v.tensor_scalar(rows[s][:, tt, :], misc[b][:, tt, :], mean_var[s][:, tt, 0:1],
                                                  rstd[s][:, tt:tt + 1], ALU.subtract, ALU.mult)
                        ins.then_inc(misc_free[b].sem, 1)
                    elif kind == "F1" and n % 2:
                        wait_misc_full(dve, i, u)
                        if a == 1 and n == 3:
                            wait_k_stacked(dve, i, s, L2)
                        for half_ in range(2):
                            m = 2 * n + half_
                            ins = v.tensor_scalar(inner[s][:, m, :], misc[b][:, half_, :],
                                                  col("b1f" if a == 1 else "b5f", m), 0.0, ALU.add, ALU.max)
                        ins.then_inc(misc_free[b].sem, 1)


def shape_constants():
    ident = np.eye(P, dtype=np.float32)
    parity = np.zeros((P, 2), np.float32)
    for r in range(96):
        parity[r, (r % 32) // 16] = 1.0
    fixed = np.zeros((32, 3, S), np.float32)
    fixed[0, 0], fixed[1, 1] = 1.0, 1.0
    fixed[2, 2] = 1.0
    return {"ident": ident, "parity": parity, "fixed": fixed}


def kernel(**inputs):
    import concourse.bacc as bacc
    from concourse.bass_utils import run_bass_kernel_spmd

    a = {n: np.asarray(v) for n, v in inputs.items()}
    l0, l1, l2, l3 = (lambda n, k=k: a[f"L{k}_xattn_{n}"] for k in range(4))
    w2 = l2("W_qkv")
    arrays = {
        "x": a["x"], "ctx": a["ctx_1024"],
        "mask0": a["mask_BxSxS2_bf0"],
        "mask1": a["mask_Bx1x1xS2_if1"].reshape(B, S),
        "mask1_cols": a["mask_Bx1x1xS2_if1"].reshape(B, QT, P).transpose(0, 2, 1),
        "mask3": a["mask_1x1xSxS_bk0"].reshape(S, S),
        "w0q": l0("Wq"), "w0k": l0("Wk"), "w0v": l0("Wv"), "w0o": l0("Wo"),
        "w1q": l1("wq"), "w1k": l1("wk"), "w1v": l1("wv"), "w1o": l1("w_out"),
        "w1f": l1("w_ff1"), "w1g": l1("w_ff2"),
        "w2q": w2[0:D].T, "w2k": w2[D:2 * D].T, "w2v": w2[2 * D:].T, "w2o": l2("W_o").T,
        "w3q": l3("sa_wq"), "w3k": l3("sa_wk"), "w3v": l3("sa_wv"), "w3o": l3("sa_wo"),
        "w4q": l3("ca_wq"), "w4k": l3("ca_wk"), "w4v": l3("ca_wv"), "w4o": l3("ca_wo"),
        "w5f": l3("ff_w1"), "w5g": l3("ff_w2"),
    }
    b2 = l2("b_qkv")
    vectors = {
        "b0q": l0("bq"), "b0k": l0("bk"), "b0v": l0("bv"), "b0o": l0("bo"), "g0": l0("gamma"), "be0": l0("beta"),
        "b1o": l1("b_out"), "g1": l1("g1"), "be1": l1("beta1"), "b1f": l1("b_ff1"), "b1g": l1("b_ff2"),
        "g2": l1("g2"), "be2": l1("beta2"),
        "b2q": b2[0:D], "b2k": b2[D:2 * D], "b2v": b2[2 * D:], "b2o": l2("b_o"),
        "g3": l2("ln_gamma"), "be3": l2("ln_beta"),
        "b3q": l3("sa_bq"), "b3k": l3("sa_bk"), "b3v": l3("sa_bv"), "b3o": l3("sa_bo"),
        "b4q": l3("ca_bq"), "b4k": l3("ca_bk"), "b4v": l3("ca_bv"), "b4o": l3("ca_bo"),
        "b5f": l3("ff_b1"), "b5g": l3("ff_b2"),
        "g4": l3("ln1_g"), "be4": l3("ln1_b"), "g5": l3("ln2_g"), "be5": l3("ln2_b"),
        "g6": l3("ln3_g"), "be6": l3("ln3_b"),
    }
    arrays["cols"] = np.concatenate([vectors[n].reshape(-1, P).T for n in COLS], axis=1)
    arrays.update(shape_constants())
    arrays = {n: np.ascontiguousarray(v) for n, v in arrays.items()}

    nc = bacc.Bacc("TRN2", target_bir_lowering=False, num_devices=1)
    t = {n: nc.dram_tensor(f"in_{n}", v.shape, mybir.dt.from_np(v.dtype), kind="ExternalInput").ap()
         for n, v in arrays.items()}
    t["out"] = nc.dram_tensor("out", (B, S, D), F32, kind="ExternalOutput").ap()
    build(nc, t)
    r = run_bass_kernel_spmd(nc, [{f"in_{n}": v for n, v in arrays.items()}], core_ids=[0])
    return r.results[0]["out"]
```
